# Optimizing a Trainium2 kernel written in Bass

```python
import numpy as np
import jax
import jax.numpy as jnp

def _softmax(x, axis=-1):
    return jax.nn.softmax(x, axis=axis)

def _gelu(x):
    return jax.nn.gelu(x, approximate=True)

def _silu(x):
    return jax.nn.silu(x)

def _sigmoid(x):
    return jax.nn.sigmoid(x)

def _layernorm(x, axis=-1, eps=1e-05):
    m = jnp.mean(x, axis=axis, keepdims=True)
    v = jnp.var(x, axis=axis, keepdims=True)
    return (x - m) / jnp.sqrt(v + eps)

def _scatter_add(tgt, idx, src, axis=0):
    return tgt.at[idx].add(src)

def _segment_sum(src, seg, n):
    return jax.ops.segment_sum(src, seg, n)
kernel_name = 'mk_adj_preln_d1_adj_r2_580e47'

def setup_inputs(seed: int=0):
    np.random.seed(seed)
    _w = jnp.asarray

    def _rec_inputs():
        import jax
        import jax.numpy as jnp
        _gk = jax.random.key(seed)
        x = -9.806e-05 + 1 * jax.random.normal(jax.random.fold_in(_gk, 1), (2048, 128), jnp.float32)
        _a = jax.random.bernoulli(jax.random.fold_in(_gk, 2), 0.0078125, (2048, 2048))
        _a = jnp.logical_or(_a, jnp.eye(2048, dtype=bool))
        _af = _a.astype(jnp.float32)
        _af = _af * jax.random.uniform(jax.random.fold_in(_gk, 3), (2048, 2048), jnp.float32, 0.05, 1)
        adj = _af
        return (x, adj)
    x, adj = _rec_inputs()

    def _L0_gnn_setup():
        import jax, jax.numpy as jnp
        import numpy as np
        N_NODE = 2048
        N_FEA_IN = 128
        N_FEA_OUT = 128
        key = jax.random.key(seed)
        k_x, k_a, k_w, k_att = jax.random.split(key, 4)
        stdv_w = 1.0 / np.sqrt(N_FEA_OUT)
        stdv_a = 1.0 / np.sqrt(2 * N_FEA_OUT)
        X = jax.random.normal(k_x, (N_NODE, N_FEA_IN), dtype=jnp.float32)
        A = jax.random.uniform(k_a, (N_NODE, N_NODE), dtype=jnp.float32)
        W = jax.random.uniform(k_w, (N_FEA_IN, N_FEA_OUT), minval=-stdv_w, maxval=stdv_w, dtype=jnp.float32)
        a = jax.random.uniform(k_att, (1, 2 * N_FEA_OUT), minval=-stdv_a, maxval=stdv_a, dtype=jnp.float32)
        return {'X': X, 'A': A, 'W': W, 'a': a}
    _L0_gnn_all = _L0_gnn_setup()
    _L0_gnn_in = {k: v for k, v in _L0_gnn_all.items() if k in ('W', 'a')}
    del _L0_gnn_all
    return {'x': x, 'adj': adj, 'L0_gnn_W': _L0_gnn_in['W'], 'L0_gnn_a': _L0_gnn_in['a']}

def reference(x, adj, L0_gnn_W, L0_gnn_a):
    import jax
    import jax.numpy as jnp

    def _L0_gnn_ref(X, A, W, a):
        import jax, jax.numpy as jnp
        import numpy as np
        N_NODE = 2048
        N_FEA_IN = 128
        N_FEA_OUT = 128
        XW = jnp.matmul(X, W)
        f = W.shape[1]
        s_col = jnp.matmul(XW, a[0, :f])
        s_row = jnp.matmul(XW, a[0, f:])
        Z1 = jax.nn.leaky_relu(s_row[:, None] + s_col[None, :], negative_slope=0.01)
        den = jnp.exp(Z1)
        num = jnp.matmul(A, den)
        att = jnp.where(num != 0, den / jnp.where(num != 0, num, 1.0), 0.0)
        H = jnp.matmul(A, jnp.matmul(att, XW))
        return H
    h = jnp.maximum(_layernorm(x, axis=-1), 0.0)
    x = x + _L0_gnn_ref(h, adj, L0_gnn_W, L0_gnn_a)
    return x

_drawn_inputs = setup_inputs


def setup_inputs(seed=0):
    import zlib

    import numpy as np

    out = dict(_drawn_inputs(seed))
    spreads = {}
    factors = {}
    for name, (base, spread) in spreads.items():
        noise = np.random.default_rng([zlib.crc32(name.encode()), seed]).standard_normal(out[name].shape)
        drawn = base * np.exp(spread * noise) if base else spread * noise
        out[name] = jnp.asarray(drawn.astype(out[name].dtype))
    for name, factor in factors.items():
        out[name] = (out[name] * factor).astype(out[name].dtype)
    return out
```

```python
from contextlib import ExitStack

import concourse.bass as bass
from concourse import mybir

ALU = mybir.AluOpType
ACT = mybir.ActivationFunctionType
F32 = mybir.dt.float32

P = 128
SLOPE = 0.01
EPS = 1e-5
CH = 512


def build_gnn(nc, x, adj, w, a, out):
    N, FI = x.shape
    FO = w.shape[1]
    assert FI == P and FO == P and N % CH == 0
    T = N // P
    C = N // CH
    G = CH // P
    FA = FO + 2
    XP = CH // 2

    x_rows = x.rearrange("(t p) f -> p t f", p=P)
    out_rows = out.rearrange("(t p) f -> p t f", p=P)
    a_halves = a.rearrange("o (h f) -> (o h) f", h=2)

    with ExitStack() as ctx:
        def sb(name, shape):
            return ctx.enter_context(nc.sbuf_tensor(name, shape, F32))

        def sem(name):
            return ctx.enter_context(nc.semaphore(name))

        ps = ctx.enter_context(nc.psum_tensor("ps", [P, 8, CH], F32))

        adj_t = sb("adj_t", [P, T, N])
        stage = sb("stage", [P, 2, N])
        shared = sb("shared", [P, 2, N])
        x_sb = shared[:, 0, :].rearrange("p (t f) -> p t f", f=P)
        h_t = shared[:, 1, :]
        den_k = shared[:, :, :].rearrange("p s (t j) -> p s t j", j=P)
        att_sum = shared[:, 1, :].rearrange("p (t f) -> p t f", f=P)
        row_bc = sb("row_bc", [P, N])
        col_bc = sb("col_bc", [P, N])
        xw = sb("xw", [P, T, FA])
        xw_now = sb("xw_now", [P, 2, FA])
        den_t = sb("den_t", [P, C, CH])
        zero_num = sb("zero_num", [P, CH])
        recip = sb("recip", [P, CH])
        ident = sb("ident", [P, P])
        w_aug = sb("w_aug", [P, FA])
        w_t = sb("w_t", [P, P])
        a_in = sb("a_in", [2, FO])
        a_t = sb("a_t", [P, 2])
        w_rep = sb("w_rep", [P, 2, P])
        ones = sb("ones", [P, P])
        stats = sb("stats", [P, T, 6])
        mean_var = sb("mean_var", [P, T, 2])
        rstd = sb("rstd", [P, T])
        std = sb("std", [P, T])
        eps_col = sb("eps_col", [P, 1])
        zeros = stage[:, 1, 0:CH]

        ld_x, ld_w, ld_a = sem("ld_x"), sem("ld_w"), sem("ld_a")
        ld_adj = [sem("ld_adj0"), sem("ld_adj1")]
        x_again = sem("x_again")
        ident_zero, ident_ok = sem("ident_zero"), sem("ident_ok")
        dve_step = sem("dve_step")
        w_turned, w_turned_sb, wa_done, wa_sb = sem("w_turned"), sem("w_turned_sb"), sem("wa_done"), sem("wa_sb")
        std_ok, var_ok, norm_ok = sem("std_ok"), sem("var_ok"), sem("norm_ok")
        h_turned, h_sb = sem("h_turned"), sem("h_sb")
        xw_done, xw_sb = sem("xw_done"), sem("xw_sb")
        bc_done, bc_sb_dve, bc_sb_act = sem("bc_done"), sem("bc_sb_dve"), sem("bc_sb_act")
        adj_turned = sem("adj_turned")
        adj_sb_dve, adj_sb_act = sem("adj_sb_dve"), sem("adj_sb_act")
        zeros_ok = sem("zeros_ok")
        z_ok, leaky_k_ok, den_k_ok = sem("z_ok"), sem("leaky_k_ok"), sem("den_k_ok")
        xw_now_ok = sem("xw_now_ok")
        z_t_ok, leaky_t_ok, den_t_ok = sem("z_t_ok"), sem("leaky_t_ok"), sem("den_t_ok")
        num_done, num_free, att_ok, att_used = sem("num_done"), sem("num_free"), sem("att_ok"), sem("att_used")
        sum_t_sb, sum_turned, sum_sb = sem("sum_t_sb"), sem("sum_turned"), sem("sum_sb")
        prod_done, prod_sb, prod_turned, res_ok = sem("prod_done"), sem("prod_sb"), sem("prod_turned"), sem("res_ok")
        stored = [sem("stored0"), sem("stored1")]

        sum_t = stage[:, 0, :]
        prod_t = stage[:, 1, 0:2 * CH].rearrange("p (s n) -> p s n", s=2)
        result = stage[:, 1, 2 * CH:4 * CH].rearrange("p (s g f) -> p s g f", s=2, f=P)

        block = ctx.enter_context(nc.Block())

        @block.sync
        def _(sp):
            sp.dma_start(x_sb, x_rows).then_inc(ld_x, 16)
            sp.dma_start(w_aug[:, 0:FO], w).then_inc(ld_w, 16)
            sp.dma_start(a_in[:], a_halves).then_inc(ld_a, 16)
            for s in range(2):
                sp.dma_start(stage[:, s, :], adj[s * P:(s + 1) * P, :]).then_inc(ld_adj[s], 16)
            with sp.Fori(1, T // 2) as j:
                for s in range(2):
                    sp.wait_ge(adj_turned, (2 * j + s - 1) * G)
                    sp.dma_start(stage[:, s, :], adj[bass.ds((2 * j + s) * P, P), :]).then_inc(ld_adj[s], 16)
            sp.wait_ge(num_done, (T - 1) * C)
            sp.dma_start(x_sb, x_rows).then_inc(x_again, 16)
            for c in range(C):
                sp.wait_ge(res_ok, c + 1)
                sp.dma_start(out_rows[:, c * G:(c + 1) * G, :], result[:, c % 2]).then_inc(stored[c % 2], 16)
            for s in range(2):
                sp.wait_ge(stored[s], 16 * C // 2)

        @block.gpsimd
        def _(pool):
            nc.gpsimd.memset(ident[:], 0.0).then_inc(ident_zero, 1)
            pool.wait_ge(ident_zero, 1)
            nc.gpsimd.affine_select(out=ident[:], in_=ident[:], compare_op=ALU.not_equal, fill=1.0, base=0,
                                    pattern=[[-1, P]], channel_multiplier=1).then_inc(ident_ok, 1)
            pool.wait_ge(xw_sb, T // 2)
            nc.gpsimd.tensor_copy(xw_now[:, 0, :], xw[:, 0, :]).then_inc(xw_now_ok, 1)
            nc.gpsimd.tensor_copy(xw_now[:, 1, :], xw[:, 1, :]).then_inc(xw_now_ok, 1)
            with pool.Fori(1, T // 2) as j:
                for s in range(2):
                    pool.wait_ge(att_used, (2 * j + s - 1) * C)
                    nc.gpsimd.tensor_copy(xw_now[:, s, :], xw[:, 2 * j + s, :]).then_inc(xw_now_ok, 1)

        @block.tensor
        def _(pe):
            pe.wait_ge(ident_ok, 1)
            pe.wait_ge(ld_w, 16)
            pe.wait_ge(ld_a, 16)
            nc.tensor.transpose(ps[:, 0, 0:P], w_aug[:, 0:FO], ident[:])
            nc.tensor.transpose(ps[:, 1, 0:2], a_in[:], ident[0:2, 0:2]).then_inc(w_turned, 1)
            pe.wait_ge(w_turned_sb, 2)
            nc.tensor.matmul(ps[:, 2, 0:2], w_t[:], a_t[:], start=True, stop=True).then_inc(wa_done, 1)
            for g in range(C):
                for k in range(G):
                    t = g * G + k
                    pe.wait_ge(norm_ok, t + 1)
                    last = nc.tensor.transpose(ps[:, 4 + g, k * P:(k + 1) * P], x_sb[:, t, :], ident[:])
                last.then_inc(h_turned, 1)
            pe.wait_ge(wa_sb, 1)
            pe.wait_ge(h_sb, C)
            for t in range(T):
                last = nc.tensor.matmul(ps[:, t // 2, (t % 2) * XP:(t % 2) * XP + FA], h_t[:, t * P:(t + 1) * P],
                                        w_aug[:], start=True, stop=True, skip_group_check=True)
                if t % 2:
                    last.then_inc(xw_done, 1)
            pe.wait_ge(wa_sb, 3)
            for b in range(2 * C):
                pe.wait_ge(xw_sb, b + 1)
                c = b % C
                nc.tensor.matmul(ps[:, b, :], w_rep[:, 1 if b < C else 0, :], h_t[:, c * CH:(c + 1) * CH],
                                 start=True, stop=True).then_inc(bc_done, 1)
            pe.wait_ge(bc_sb_dve, C)
            pe.wait_ge(bc_sb_act, C)

            def turn_rows(r, s, first):
                pe.wait_ge(ld_adj[s], (r // 2 + 1) * 16 if isinstance(r, int) else (r - s) * 8 + 16)
                for g in range(C):
                    if not first:
                        if g % 2:
                            pe.wait_ge(adj_sb_act, (r - 1) * 2 - 2 + g // 2 + 1)
                        else:
                            pe.wait_ge(adj_sb_dve, (r - 1) * 2 - 2 + g // 2 + 1)
                    for k in range(G):
                        t = g * G + k
                        last = nc.tensor.transpose(ps[:, C * s + g, k * P:(k + 1) * P], stage[:, s, t * P:(t + 1) * P],
                                                   ident[:])
                    last.then_inc(adj_turned, 1)

            turn_rows(0, 0, True)
            turn_rows(1, 1, True)
            with pe.Fori(1, T // 2) as j:
                for s in range(2):
                    turn_rows(2 * j + s, s, False)

            pe.wait_ge(adj_sb_act, T * 2)
            pe.wait_ge(adj_sb_dve, T * 2)
            pe.wait_ge(zeros_ok, 1)
            for c in range(C):
                nc.tensor.matmul(ps[:, C + c, :], zeros[:, 0:P], zeros, start=True, stop=False,
                                 skip_group_check=True)

            def num(b, s, c, first=False):
                if c == 0:
                    pe.wait_ge(den_k_ok, b + 1)
                if not first:
                    pe.wait_ge(num_free, b * C + c - C + 1)
                for t in range(T):
                    last = nc.tensor.matmul(ps[:, c, :], den_k[:, s, t, :], adj_t[:, t, c * CH:(c + 1) * CH],
                                            start=(t == 0), stop=(t == T - 1))
                last.then_inc(num_done, 1)

            def gather(b, s, c):
                if c == 0:
                    pe.wait_ge(xw_now_ok, b + 1)
                pe.wait_ge(att_ok, b * C + c + 1)
                nc.tensor.matmul(ps[:, C + c, :], xw_now[:, s, 0:FO], den_t[:, c, :], start=False, stop=False,
                                 skip_group_check=True).then_inc(att_used, 1)

            def pe_block(b, s, first, last):
                for c in range(1, C):
                    num(b, s, c, first)
                    gather(b, s, c - 1)
                if not last:
                    num(b + 1, 1 - s, 0)
                gather(b, s, C - 1)

            num(0, 0, 0, True)
            pe_block(0, 0, True, False)
            pe_block(1, 1, False, False)
            with pe.Fori(1, T // 2 - 1) as j:
                pe_block(2 * j, 0, False, False)
                pe_block(2 * j + 1, 1, False, False)
            pe_block(T - 2, 0, False, False)
            pe_block(T - 1, 1, False, True)

            for g in range(C):
                pe.wait_ge(sum_t_sb, g + 1)
                for k in range(G):
                    t = g * G + k
                    last = nc.tensor.transpose(ps[:, g, k * P:(k + 1) * P], sum_t[:, t * P:(t + 1) * P], ident[:])
                last.then_inc(sum_turned, 1)
            pe.wait_ge(sum_sb, C)

            def turn_product(c):
                pe.wait_ge(prod_sb, c + 1)
                if c >= 2:
                    pe.wait_ge(res_ok, c - 1)
                for k in range(G):
                    last = nc.tensor.transpose(ps[:, c % 2, k * P:(k + 1) * P], prod_t[:, c % 2, k * P:(k + 1) * P],
                                               ident[:])
                last.then_inc(prod_turned, 1)

            for c in range(C):
                for t in range(T):
                    last = nc.tensor.matmul(ps[:, C + c, :], att_sum[:, t, :], adj_t[:, t, c * CH:(c + 1) * CH],
                                            start=(t == 0), stop=(t == T - 1))
                last.then_inc(prod_done, 1)
                if c:
                    turn_product(c - 1)
            turn_product(C - 1)

        @block.scalar
        def _(act):
            act.wait_ge(var_ok, T + 1)
            nc.scalar.activation(std[:], mean_var[:, :, 1], ACT.Sqrt, bias=eps_col[:]).then_inc(std_ok, 1)
            for c in range(C):
                act.wait_ge(bc_done, C + c + 1)
                nc.scalar.copy(col_bc[:, c * CH:(c + 1) * CH], ps[:, C + c, :]).then_inc(bc_sb_act, 1)

            def copy_turned(r, s):
                for g in range(1, C, 2):
                    act.wait_ge(adj_turned, r * C + g + 1)
                    nc.scalar.copy(adj_t[:, g * G:(g + 1) * G, bass.ds(r * P, P)],
                                   ps[:, C * s + g, :].rearrange("p (k i) -> p k i", k=G)).then_inc(adj_sb_act, 1)

            with act.Fori(0, T // 2) as j:
                for s in range(2):
                    copy_turned(2 * j + s, s)

            def exp_block(b, s):
                act.wait_ge(leaky_k_ok, b + 1)
                nc.scalar.activation(shared[:, s, :], shared[:, s, :], ACT.Exp).then_inc(den_k_ok, 1)

            def exp_turned(b, c):
                act.wait_ge(leaky_t_ok, b * C + c + 1)
                nc.scalar.activation(den_t[:, c, :], den_t[:, c, :], ACT.Exp).then_inc(den_t_ok, 1)

            def act_block(b, s, first):
                exp_turned(b, C - 1)
                exp_turned(b + 1, 0)
                if not first:
                    exp_block(b + 1, 1 - s)
                for c in range(1, C - 1):
                    exp_turned(b + 1, c)

            exp_block(0, 0)
            exp_block(1, 1)
            for c in range(C - 1):
                exp_turned(0, c)
            act_block(0, 0, True)
            with act.Fori(0, T // 2 - 1) as j:
                act_block(2 * j + 1, 1, False)
                act_block(2 * j + 2, 0, False)
            exp_turned(T - 1, C - 1)

            for c in range(C):
                act.wait_ge(prod_done, c + 1)
                if c >= 2:
                    act.wait_ge(prod_turned, c - 1)
                nc.scalar.copy(prod_t[:, c % 2, :], ps[:, C + c, :]).then_inc(prod_sb, 1)

        @block.vector
        def _(dve):
            nc.vector.memset(eps_col[:], EPS).then_inc(var_ok, 1)
            nc.vector.memset(ones[:], 1.0).then_inc(dve_step, 1)
            dve.wait_ge(ld_x, 16)
            for t in range(T):
                nc.vector.bn_stats(stats[:, t, :], x_sb[:, t, :]).then_inc(dve_step, 1)
            for t in range(T):
                dve.wait_ge(dve_step, t + 2)
                nc.vector.bn_aggr(mean_var[:, t, :], stats[:, t, :]).then_inc(var_ok, 1)
            dve.wait_ge(w_turned, 1)
            nc.vector.tensor_copy(w_t[:], ps[:, 0, 0:P]).then_inc(w_turned_sb, 1)
            nc.vector.tensor_copy(a_t[:], ps[:, 1, 0:2]).then_inc(w_turned_sb, 1)
            dve.wait_ge(std_ok, 1)
            nc.vector.reciprocal(rstd[:], std[:]).then_inc(dve_step, 1)
            dve.wait_ge(dve_step, T + 2)
            for t in range(T):
                nc.vector.tensor_scalar(x_sb[:, t, :], x_sb[:, t, :], mean_var[:, t, 0:1], rstd[:, t:t + 1],
                                        ALU.subtract, ALU.mult).then_inc(norm_ok, 1)
            dve.wait_ge(wa_done, 1)
            nc.vector.tensor_copy(w_aug[:, FO:FA], ps[:, 2, 0:2]).then_inc(wa_sb, 1)
            dve.wait_ge(wa_sb, 1)
            for h in range(2):
                nc.vector.tensor_scalar(w_rep[:, h, :], ones[:], w_aug[:, FO + h:FO + h + 1], None,
                                        ALU.mult).then_inc(wa_sb, 1)
            for g in range(C):
                dve.wait_ge(h_turned, g + 1)
                nc.vector.tensor_scalar(h_t[:, g * CH:(g + 1) * CH], ps[:, C + g, :], 0.0, None,
                                        ALU.max).then_inc(h_sb, 1)
            for b in range(T // 2):
                dve.wait_ge(xw_done, b + 1)
                pair = ps[:, b, :].rearrange("p (k n) -> p k n", k=2)
                nc.vector.tensor_copy(xw[:, 2 * b:2 * b + 2, :], pair[:, :, 0:FA]).then_inc(xw_sb, 1)
            for c in range(C):
                dve.wait_ge(bc_done, c + 1)
                nc.vector.tensor_copy(row_bc[:, c * CH:(c + 1) * CH], ps[:, c, :]).then_inc(bc_sb_dve, 1)

            def scores(b, s, first=False):
                if not first:
                    dve.wait_ge(num_done, (b - 1) * C)
                nc.vector.tensor_tensor(den_k[:, s], xw[:, :, FO + 1:FA].broadcast_to((P, T, P)),
                                        col_bc[:, bass.ds(b * P, P)].unsqueeze(1).broadcast_to((P, T, P)),
                                        ALU.add).then_inc(z_ok, 1)
                dve.wait_ge(z_ok, b + 1)
                nc.vector.scalar_tensor_tensor(out=shared[:, s, :], in0=shared[:, s, :], scalar=SLOPE,
                                               in1=shared[:, s, :], op0=ALU.mult, op1=ALU.max).then_inc(leaky_k_ok, 1)

            def scores_turned(b, s, c, first=False):
                q = b * C + c
                dve.wait_ge(xw_now_ok, b + 1)
                if not first:
                    dve.wait_ge(att_used, q - C + 1)
                nc.vector.tensor_scalar(den_t[:, c, :], row_bc[:, c * CH:(c + 1) * CH], xw_now[:, s, FO:FO + 1], None,
                                        ALU.add).then_inc(z_t_ok, 1)
                dve.wait_ge(z_t_ok, q + 1)
                nc.vector.scalar_tensor_tensor(out=den_t[:, c, :], in0=den_t[:, c, :], scalar=SLOPE,
                                               in1=den_t[:, c, :], op0=ALU.mult, op1=ALU.max).then_inc(leaky_t_ok, 1)

            def copy_turned(r, s):
                for g in range(0, C, 2):
                    dve.wait_ge(adj_turned, r * C + g + 1)
                    nc.vector.tensor_copy(adj_t[:, g * G:(g + 1) * G, bass.ds(r * P, P)],
                                          ps[:, C * s + g, :].rearrange("p (k i) -> p k i", k=G)).then_inc(adj_sb_dve, 1)

            with dve.Fori(0, T // 2) as j:
                for s in range(2):
                    copy_turned(2 * j + s, s)
            dve.wait_ge(xw_sb, T // 2)
            dve.wait_ge(bc_done, 2 * C)
            dve.wait_ge(bc_sb_act, C)
            scores(0, 0, True)
            scores(1, 1, True)
            dve.wait_ge(adj_turned, T * C)
            nc.vector.memset(zeros, 0.0).then_inc(zeros_ok, 1)

            def attention(b, c):
                q = b * C + c
                dve.wait_ge(num_done, q + 1)
                nc.vector.tensor_scalar(zero_num[:], ps[:, c, :], 0.0, None, ALU.is_equal).then_inc(dve_step, 1)
                dve.wait_ge(dve_step, q * 3 + T + 3)
                nc.vector.tensor_tensor(recip[:], ps[:, c, :], zero_num[:], ALU.add).then_inc(num_free, 1)
                dve.wait_ge(num_free, q + 1)
                nc.vector.reciprocal(recip[:], recip[:]).then_inc(dve_step, 1)
                dve.wait_ge(dve_step, q * 3 + T + 4)
                nc.vector.scalar_tensor_tensor(out=recip[:], in0=zero_num[:], scalar=0.0, in1=recip[:],
                                               op0=ALU.is_equal, op1=ALU.mult).then_inc(dve_step, 1)
                dve.wait_ge(dve_step, q * 3 + T + 5)
                dve.wait_ge(den_t_ok, q + 1)
                nc.vector.tensor_tensor(den_t[:, c, :], den_t[:, c, :], recip[:], ALU.mult).then_inc(att_ok, 1)

            def dve_block(b, s, first, last):
                for c in range(C):
                    attention(b, c)
                    if c == 0:
                        scores_turned(b, s, C - 1, first)
                    elif not last:
                        scores_turned(b + 1, 1 - s, c - 1)
                    if c == 1 and not last and not first:
                        scores(b + 1, 1 - s)

            for c in range(C - 1):
                scores_turned(0, 0, c, True)
            dve_block(0, 0, True, False)
            dve_block(1, 1, False, False)
            with dve.Fori(1, T // 2 - 1) as j:
                dve_block(2 * j, 0, False, False)
                dve_block(2 * j + 1, 1, False, False)
            dve_block(T - 2, 0, False, False)
            dve_block(T - 1, 1, False, True)

            for c in range(C):
                dve.wait_ge(att_used, (T - 1) * C + c + 1)
                nc.vector.tensor_copy(sum_t[:, c * CH:(c + 1) * CH], ps[:, C + c, :]).then_inc(sum_t_sb, 1)
            dve.wait_ge(num_done, T * C)
            for g in range(C):
                dve.wait_ge(sum_turned, g + 1)
                nc.vector.tensor_copy(att_sum[:, g * G:(g + 1) * G, :],
                                      ps[:, g, :].rearrange("p (k f) -> p k f", k=G)).then_inc(sum_sb, 1)
            dve.wait_ge(x_again, 16)
            for c in range(C):
                dve.wait_ge(prod_turned, c + 1)
                if c >= 2:
                    dve.wait_ge(stored[c % 2], 16)
                nc.vector.tensor_tensor(result[:, c % 2], ps[:, c % 2, :].rearrange("p (k f) -> p k f", k=G),
                                        x_sb[:, c * G:(c + 1) * G, :], ALU.add).then_inc(res_ok, 1)


_INS = ["x", "adj", "L0_gnn_W", "L0_gnn_a"]


def kernel(**inputs):
    import numpy as _np
    import concourse.bacc as _bacc
    from concourse import mybir as _mybir
    from concourse.bass_utils import run_bass_kernel_spmd as _run

    nc = _bacc.Bacc("TRN2", target_bir_lowering=False, num_devices=1)
    arrays, args = {}, []
    for name in _INS:
        v = _np.ascontiguousarray(inputs[name])
        arrays[f"in_{name}"] = v
        args.append(nc.dram_tensor(f"in_{name}", v.shape, _mybir.dt.from_np(v.dtype), kind="ExternalInput").ap())
    out = nc.dram_tensor("out", inputs["x"].shape, _mybir.dt.float32, kind="ExternalOutput").ap()
    build_gnn(nc, *args, out)
    r = _run(nc, [arrays], core_ids=[0])
    return r.results[0]["out"]
```

```python
from contextlib import ExitStack

import concourse.bass as bass
from concourse import mybir


ALU = mybir.AluOpType
ACT = mybir.ActivationFunctionType
AX_X = mybir.AxisListType.X
F32 = mybir.dt.float32
BF16 = mybir.dt.bfloat16
U32 = mybir.dt.uint32
I32 = mybir.dt.int32

P = 128
SLOPE = 0.01
STEEP = 1.0 - SLOPE
EPS = 1e-5
CH = 512
TINY = 1e-19


def build_gnn(nc, x, adj, w, a, out):
    N, FI = x.shape
    FO = w.shape[1]
    assert FI == P and FO == P and N % (4 * CH) == 0
    T = N // P
    C = N // CH
    G = CH // P
    FA = FO + 2
    COL_C, COL_S, COL_W, FX = FO, FO + 1, FO + 2, FO + 3
    XP = CH // 2
    R = P - 2
    S = (N + R * T) // R
    assert S == 2 * T
    LAG = 2
    RING = 4
    H = N // 2

    x_rows = x.rearrange("(t p) f -> p t f", p=P)
    out_rows = out.rearrange("(t p) f -> p t f", p=P)
    a_halves = a.rearrange("o (h f) -> (o h) f", h=2)

    with ExitStack() as ctx:
        def sb(name, shape, dt=F32):
            return ctx.enter_context(nc.sbuf_tensor(name, shape, dt))

        def sem(name):
            return ctx.enter_context(nc.semaphore(name))

        adj_t_dram = nc.dram_tensor("adj_t_dram", (N + 2 * T, N), F32, kind="Internal").ap()
        adj_t_rows = adj_t_dram[0:N, :].rearrange("(t p) i -> p t i", p=P)
        table_dram = nc.dram_tensor("table_dram", (N, FX), F32, kind="Internal").ap()

        ps = ctx.enter_context(nc.psum_tensor("ps", [P, 8, CH], F32))

        big = sb("big", [P, T, N])
        ring = sb("ring", [P, RING, N])
        row_bc = sb("row_bc", [P, N])
        reg_w = sb("reg_w", [P, N])
        reg_sq = sb("reg_sq", [P, N])
        reg_n = sb("reg_n", [P, N])
        table = sb("table", [P, T, FX])

        x_sb = reg_w[:, :].rearrange("p (t f) -> p t f", f=P)
        pick_row = reg_w[:, :].rearrange("p (t r) -> p t r", r=P)
        w_bc = reg_w
        h_t = reg_sq
        compared = [reg_sq[:, k * H:(k + 1) * H].bitcast(BF16) for k in range(2)]
        diag = reg_sq[:, :].rearrange("p (t r) -> p t r", r=P)
        square = reg_sq
        col_bc = reg_n
        att_num = reg_n

        used = [0]

        def temp(*shape):
            n = 1
            for d in shape:
                n *= d
            at = used[0]
            used[0] += n
            assert used[0] <= N
            v = reg_n[:, at:at + n]
            if len(shape) == 2:
                v = v.rearrange("p (a b) -> p a b", b=shape[1])
            return v

        ident = sb("ident", [P, P])
        ones = sb("ones", [P, P])
        w_aug = sb("w_aug", [P, FA])
        iota_step = sb("iota_step", [P, S])
        iota_tile = sb("iota_tile", [P, T])
        iota_chunk = sb("iota_chunk", [P, T])
        node = sb("node", [P, T])
        prow = sb("prow", [P, 1])
        row_flag = sb("row_flag", [P, 4])
        a_t = sb("a_t", [P, 2])
        s_nat = sb("s_nat", [P, T])
        c_nat = sb("c_nat", [P, T])
        p_nat = sb("p_nat", [P, T])
        gp_nat = sb("gp_nat", [P, T])
        smax = sb("smax", [P, 1])
        shift = sb("shift", [P, 2])
        eps_col = sb("eps_col", [P, 2])
        counts = sb("counts", [P, 4, T])
        rank = sb("rank", [P, T])
        rank_u = sb("rank_u", [P, T], U32)
        slot_idx = sb("slot_idx", [P, S], U32)
        slot_gp = sb("slot_gp", [P, S])
        slot_p = sb("slot_p", [P, S])
        block_of = sb("block_of", [P, S])
        block_int = sb("block_int", [P, S], I32)
        goes_on = sb("goes_on", [P, S])
        den_now = sb("den_now", [P, 2, P])
        xw_now = sb("xw_now", [P, RING, FO])
        before, after, iota_row, w_rep = [xw_now[:, k, :] for k in range(4)]
        bound_in = temp(T)
        member_ext = temp(T, T + 1)
        member = temp(T, T)
        member_flat = member.rearrange("p a b -> p (a b)")
        carry_w = temp(T, 2 * T)
        in_step = reg_sq[:, 0:T * S].rearrange("p (t s) -> p t s", s=S)
        pick_step = reg_sq[:, T * S:4 * T * S].rearrange("p (t n) -> p t n", n=3 * S)
        w_t = den_now[:, 0, :]
        a_in = den_now[0:2, 1, :]
        c_diag = ring[:, 3, :].rearrange("p (t r) -> p t r", r=P)
        stats = ring[:, 3, 0:6 * T].rearrange("p (t n) -> p t n", n=6)
        mean_var = ring[:, 3, 6 * T:8 * T].rearrange("p (t n) -> p t n", n=2)
        std = ring[:, 3, 8 * T:9 * T]
        rstd = ring[:, 3, 9 * T:10 * T]
        zeros = ring[:, 3, 0:CH]
        PAD = T // 2
        totals = [ring[:, 3, CH + k * (PAD + T) * T:CH + (k + 1) * (PAD + T) * T].rearrange("p (t b) -> p t b", b=T)
                  for k in range(2)]
        wide = ring[:, 3, N - 2 * CH + 256:N - CH + 256].rearrange("p (s b) -> p s b", b=T)
        tied = ring[:, 3, N - P:N].bitcast(BF16)
        carry_sb = ring[0:2 * T, 0, :]

        sum_t = ring[:, 0, :]
        x_again = ring[:, 1, :].rearrange("p (t f) -> p t f", f=P)
        att_sum = ring[:, 2, :].rearrange("p (t f) -> p t f", f=P)
        prod_t = ring[:, 3, 0:2 * CH].rearrange("p (s n) -> p s n", s=2)
        result = ring[:, 3, 2 * CH:4 * CH].rearrange("p (s g f) -> p s g f", s=2, f=P)

        names = """ld_x ld_w ld_a ident_zero consts tri_ok w_turned w_turned_sb wa_done wa_sb std_ok var_ok norm_ok
            h_turned h_sb xw_done xw_sb c_diag_ok bc_done bc_sb_dve bc_sb_act adj_turned adj_sb adj_t_stored dve_step
            smax_ok exps_ok w_in_table rank_ok table_stored table_loaded bound_in_ok bound_done prefix_done weights_ok
            carry_done carry_sb_ok carry_stored pick_ok pick_done slots_ok diag_ok w_bc_done w_bc_ok
            den_ok num_done num_added squared logged recip_ok numer_ok signed_ok att_ok
            xw_now_ok att_used x_loaded sum_t_sb sum_turned sum_sb prod_done prod_sb prod_turned res_ok""".split()
        sems = {n: sem(n) for n in names}
        (ld_x, ld_w, ld_a, ident_zero, consts, tri_ok, w_turned, w_turned_sb, wa_done, wa_sb, std_ok, var_ok, norm_ok,
         h_turned, h_sb, xw_done, xw_sb, c_diag_ok, bc_done, bc_sb_dve, bc_sb_act, adj_turned, adj_sb, adj_t_stored, dve_step,
         smax_ok, exps_ok, w_in_table, rank_ok, table_stored, table_loaded, bound_in_ok, bound_done, prefix_done, weights_ok,
         carry_done, carry_sb_ok, carry_stored, pick_ok, pick_done, slots_ok, diag_ok, w_bc_done, w_bc_ok,
         den_ok, num_done, num_added, squared, logged, recip_ok, numer_ok, signed_ok, att_ok,
         xw_now_ok, att_used, x_loaded, sum_t_sb, sum_turned, sum_sb, prod_done, prod_sb, prod_turned,
         res_ok) = [sems[n] for n in names]
        ld_adj = [sem(f"ld_adj{s}") for s in range(RING - 1)]
        gathered = [sem(f"gathered{s}") for s in range(RING)]
        reloaded = [sem(f"reloaded{t}") for t in range(T)]
        stored = [sem("stored0"), sem("stored1")]
        AR = RING - 1

        block = ctx.enter_context(nc.Block())

        @block.sync
        def _(sp):
            sp.dma_start(x_sb, x_rows).then_inc(ld_x, 16)
            sp.dma_start(w_aug[:, 0:FO], w).then_inc(ld_w, 16)
            sp.dma_start(a_in, a_halves).then_inc(ld_a, 16)
            for r in range(T):
                s = r % AR
                if r >= AR:
                    sp.wait_ge(adj_turned, (r - AR + 1) * C)
                sp.dma_start(ring[:, s, :], adj[r * P:(r + 1) * P, :]).then_inc(ld_adj[s], 16)
            sp.wait_ge(table_stored, 16 * T)
            sp.dma_start(table[:], table_dram.rearrange("(t p) f -> p t f", p=P)).then_inc(table_loaded, 16)
            sp.wait_ge(carry_sb_ok, C)
            sp.dma_start(adj_t_dram[N:N + 2 * T, :], carry_sb).then_inc(carry_stored, 16)
            for t in range(T):
                sp.wait_ge(att_used, t * C + C)
                sp.dma_start(big[:, t, :], adj_t_dram[t * P:(t + 1) * P, :]).then_inc(reloaded[t], 16)
            sp.wait_ge(num_done, S * C)
            sp.dma_start(x_again, x_rows).then_inc(x_loaded, 16)
            for c in range(C):
                sp.wait_ge(res_ok, c + 1)
                sp.dma_start(out_rows[:, c * G:(c + 1) * G, :], result[:, c % 2]).then_inc(stored[c % 2], 16)
            for s in range(2):
                sp.wait_ge(stored[s], 16 * C // 2)

        @block.gpsimd
        def _(pool):
            nc.gpsimd.memset(ident[:], 0.0).then_inc(ident_zero, 1)
            nc.gpsimd.memset(ones[:], 1.0).then_inc(ident_zero, 1)
            pool.wait_ge(ident_zero, 2)
            nc.gpsimd.affine_select(out=ident[:], in_=ident[:], compare_op=ALU.not_equal, fill=1.0, base=0,
                                    pattern=[[-1, P]], channel_multiplier=1).then_inc(consts, 1)
            nc.gpsimd.affine_select(out=before, in_=ones[:], compare_op=ALU.is_gt, fill=0.0, base=0,
                                    pattern=[[1, P]], channel_multiplier=-1).then_inc(tri_ok, 1)
            nc.gpsimd.affine_select(out=after, in_=ones[:], compare_op=ALU.is_gt, fill=0.0, base=0,
                                    pattern=[[-1, P]], channel_multiplier=1).then_inc(tri_ok, 1)
            for t, base, step, mult in ((iota_row, 0, 1, 0), (iota_step, 0, 1, 0), (iota_tile, 0, P, 0),
                                        (iota_chunk, R, R, 0), (node, 0, P, 1), (prow, 0, 0, 1)):
                nc.gpsimd.iota(t[:, :], pattern=[[step, t.shape[1]]], base=base, channel_multiplier=mult,
                               allow_small_or_imprecise_dtypes=True).then_inc(tri_ok, 1)
            pool.wait_ge(rank_ok, 1)
            pool.wait_ge(w_in_table, 1)
            for t in range(T):
                nc.gpsimd.indirect_dma_start(
                    out=table_dram, out_offset=bass.IndirectOffsetOnAxis(ap=rank_u[:, t:t + 1], axis=0),
                    in_=table[:, t, :], in_offset=None).then_inc(table_stored, 16)
            pool.wait_ge(adj_t_stored, 16 * C)
            pool.wait_ge(carry_stored, 16)
            pool.wait_ge(slots_ok, 1)

            def gather(s):
                if s >= RING:
                    pool.wait_ge(num_done, (s - RING) * C + C)
                nc.gpsimd.indirect_dma_start(
                    out=ring[:, s % RING, :], out_offset=None, in_=adj_t_dram,
                    in_offset=bass.IndirectOffsetOnAxis(ap=slot_idx[:, s:s + 1], axis=0)).then_inc(
                        gathered[s % RING], 16)

            def numerator(J):
                pool.wait_ge(num_added, (J + T) * C + C)
                for h in range(2):
                    pool.wait_ge(numer_ok, 2 * J + h + 1)
                    nc.gpsimd.tensor_tensor(att_num[:, h * H:(h + 1) * H], att_num[:, h * H:(h + 1) * H],
                                            big[:, J, h * H:(h + 1) * H],
                                            ALU.mult).then_inc(signed_ok, 1)

            def xw_copy(J):
                if J >= RING:
                    pool.wait_ge(att_used, (J - RING) * C + C)
                nc.gpsimd.tensor_copy(xw_now[:, J % RING, :], table[:, J, 0:FO]).then_inc(xw_now_ok, 1)

            pool.wait_ge(w_bc_done, C + 1)
            pool.wait_ge(table_loaded, 16)
            for s in range(RING):
                gather(s)
            for J in range(RING):
                xw_copy(J)
            for s in range(RING, T + RING):
                gather(s)
            for J in range(T):
                if J >= RING:
                    xw_copy(J)
                numerator(J)
                if J + T + RING < S:
                    gather(J + T + RING)

        @block.tensor
        def _(pe):
            pe.wait_ge(consts, 1)
            pe.wait_ge(ld_w, 16)
            pe.wait_ge(ld_a, 16)
            nc.tensor.transpose(ps[:, 0, 0:P], w_aug[:, 0:FO], ident[:])
            nc.tensor.transpose(ps[:, 1, 0:2], a_in, ident[0:2, 0:2]).then_inc(w_turned, 1)
            pe.wait_ge(w_turned_sb, 2)
            nc.tensor.matmul(ps[:, 2, 0:2], w_t, a_t[:], start=True, stop=True).then_inc(wa_done, 1)
            for g in range(C):
                for k in range(G):
                    t = g * G + k
                    pe.wait_ge(norm_ok, t + 1)
                    last = nc.tensor.transpose(ps[:, 4 + g, k * P:(k + 1) * P], x_sb[:, t, :], ident[:])
                last.then_inc(h_turned, 1)
            pe.wait_ge(wa_sb, 1)
            pe.wait_ge(h_sb, C)
            for t in range(T):
                last = nc.tensor.matmul(ps[:, t // 2, (t % 2) * XP:(t % 2) * XP + FA], h_t[:, t * P:(t + 1) * P],
                                        w_aug[:], start=True, stop=True, skip_group_check=True)
                if t % 2:
                    last.then_inc(xw_done, 1)
            pe.wait_ge(wa_sb, 2)
            for b in range(2 * C):
                pe.wait_ge(xw_sb, b + 1)
                c = b % C
                if b >= C:
                    nc.tensor.matmul(ps[:, b, :], w_rep, h_t[:, c * CH:(c + 1) * CH], start=True,
                                     stop=True).then_inc(bc_done, 1)
            pe.wait_ge(c_diag_ok, 1)
            for c in range(C):
                nc.tensor.matmul(ps[:, c, :], ones[:], c_diag[:, c * G:(c + 1) * G, :], start=True,
                                 stop=True).then_inc(bc_done, 1)

            pe.wait_ge(bc_sb_dve, C)
            pe.wait_ge(bc_sb_act, C)
            for r in range(T):
                pe.wait_ge(ld_adj[r % AR], (r // AR + 1) * 16)
                for g in range(C):
                    u = r * C + g
                    if u >= 8:
                        pe.wait_ge(adj_sb, u - 7)
                    for k in range(G):
                        t = g * G + k
                        last = nc.tensor.transpose(ps[:, u % 8, k * P:(k + 1) * P],
                                                   ring[:, r % AR, t * P:(t + 1) * P], ident[:])
                    last.then_inc(adj_turned, 1)

            pe.wait_ge(adj_sb, T * C)
            pe.wait_ge(tri_ok, 2)
            pe.wait_ge(bound_in_ok, 1)
            nc.tensor.matmul(ps[:, 0, 0:T], ones[:], bound_in, start=True, stop=True).then_inc(bound_done, 1)
            pe.wait_ge(weights_ok, 1)
            nc.tensor.matmul(ps[:, 1, 0:T * T], before, member_flat, start=True, stop=True)
            nc.tensor.matmul(ps[:, 2, 0:T * T], ones[:], member_flat, start=True, stop=True).then_inc(prefix_done, 1)

            def carries(c):
                for t in range(T):
                    last = nc.tensor.matmul(ps[0:2 * T, C + c, :], carry_w[:, t, :], big[:, t, c * CH:(c + 1) * CH],
                                            start=(t == 0), stop=(t == T - 1))
                last.then_inc(carry_done, 1)

            pe.wait_ge(weights_ok, 3)
            carries(0)
            pe.wait_ge(pick_ok, 1)
            for t in range(T):
                last = nc.tensor.matmul(ps[:, 3, 0:3 * S], pick_row[:, t, :], pick_step[:, t, :],
                                        start=(t == 0), stop=(t == T - 1))
            last.then_inc(pick_done, 1)
            for c in range(1, C):
                carries(c)
            pe.wait_ge(slots_ok, 1)
            pe.wait_ge(diag_ok, 1)
            for c in range(C):
                nc.tensor.matmul(ps[:, c, :], ones[:], diag[:, c * G:(c + 1) * G, :], start=True,
                                 stop=True).then_inc(w_bc_done, 1)
            pe.wait_ge(carry_sb_ok, C)
            pe.wait_ge(pick_ok, 1)
            for c in range(C):
                last = nc.tensor.matmul(ps[:, C + c, :], zeros[:, 0:P], zeros, start=True, stop=False,
                                        skip_group_check=True)
            last.then_inc(w_bc_done, 1)
            pe.wait_ge(w_bc_ok, C)

            def slots(s, k, c, first=False):
                if c == 0:
                    pe.wait_ge(den_ok, s + 1)
                    pe.wait_ge(gathered[k], (s - k) * (16 // RING) + 16)
                if not first:
                    pe.wait_ge(num_added, s * C + c - C + 1)
                nc.tensor.matmul(ps[:, c, :], den_now[:, k % 2, :], ring[:, k, c * CH:(c + 1) * CH],
                                 start=True, stop=True).then_inc(num_done, 1)

            def product(J, s, c):
                if c == 0:
                    pe.wait_ge(xw_now_ok, J + 1)
                    pe.wait_ge(att_ok, 2 * J + 1)
                if c == C // 2:
                    pe.wait_ge(att_ok, 2 * J + 2)
                nc.tensor.matmul(ps[:, C + c, :], xw_now[:, s, :],
                                 big[:, J, c * CH:(c + 1) * CH],
                                 start=False, stop=False, skip_group_check=True).then_inc(att_used, 1)

            for s in range(RING):
                for c in range(C):
                    slots(s, s, c, s == 0)
            with pe.Fori(1, T // RING) as q:
                for k in range(RING):
                    for c in range(C):
                        slots(q * RING + k, k, c)
            for s in range(T, T + LAG):
                for c in range(C):
                    slots(s, s % RING, c)
            with pe.Fori(0, (T - RING) // RING) as q:
                for k in range(RING):
                    for c in range(C):
                        slots(T + LAG + q * RING + k, (LAG + k) % RING, c)
                        product(q * RING + k, k, c)
            for s in range(S - LAG, S):
                for c in range(C):
                    slots(s, s % RING, c)
                    product(s - T - LAG, (s - T - LAG) % RING, c)
            for J in range(T - LAG, T):
                for c in range(C):
                    product(J, J % RING, c)

            for g in range(C):
                pe.wait_ge(sum_t_sb, g + 1)
                for k in range(G):
                    t = g * G + k
                    last = nc.tensor.transpose(ps[:, g, k * P:(k + 1) * P], sum_t[:, t * P:(t + 1) * P], ident[:])
                last.then_inc(sum_turned, 1)
            for t in range(T):
                pe.wait_ge(sum_sb, t // G + 1)
                pe.wait_ge(reloaded[t], 16)
                for c in range(C):
                    last = nc.tensor.matmul(ps[:, C + c, :], att_sum[:, t, :], big[:, t, c * CH:(c + 1) * CH],
                                            start=(t == 0), stop=(t == T - 1))
                    if t == T - 1:
                        last.then_inc(prod_done, 1)
            for c in range(C):
                pe.wait_ge(prod_sb, c + 1)
                if c >= 2:
                    pe.wait_ge(res_ok, c - 1)
                for k in range(G):
                    last = nc.tensor.transpose(ps[:, c % 2, k * P:(k + 1) * P], prod_t[:, c % 2, k * P:(k + 1) * P],
                                               ident[:])
                last.then_inc(prod_turned, 1)

        @block.scalar
        def _(act):
            act.wait_ge(var_ok, T + 1)
            nc.scalar.activation(std, mean_var[:, :, 1], ACT.Sqrt, bias=eps_col[:, 0:1]).then_inc(std_ok, 1)
            for c in range(C):
                act.wait_ge(bc_done, c + 1)
                nc.scalar.copy(row_bc[:, c * CH:(c + 1) * CH], ps[:, C + c, :]).then_inc(bc_sb_act, 1)

            def copy_turned(u):
                r, g = u // C, u % C
                act.wait_ge(adj_turned, u + 1)
                nc.scalar.copy(big[:, g * G:(g + 1) * G, r * P:(r + 1) * P],
                               ps[:, u % 8, :].rearrange("p (k i) -> p k i", k=G)).then_inc(adj_sb, 1)
                if (u + 1) % (G * C) == 0:
                    q = u // (G * C)
                    act.wait_ge(adj_sb, u + 1)
                    act.dma_start(adj_t_rows[:, :, q * CH:(q + 1) * CH], big[:, :, q * CH:(q + 1) * CH]).then_inc(
                        adj_t_stored, 16)

            for u in range(8):
                copy_turned(u)
            act.wait_ge(smax_ok, 4)
            nc.scalar.activation(p_nat[:], s_nat[:], ACT.Exp, scale=SLOPE).then_inc(exps_ok, 1)
            nc.scalar.activation(gp_nat[:], s_nat[:], ACT.Exp, scale=STEEP, bias=shift[:, 1:2]).then_inc(exps_ok, 1)
            nc.scalar.activation(table[:, :, COL_W], c_nat[:], ACT.Exp, scale=STEEP,
                                 bias=shift[:, 0:1]).then_inc(w_in_table, 1)
            nc.scalar.activation(row_bc[:], row_bc[:], ACT.Exp, scale=STEEP, bias=shift[:, 1:2]).then_inc(exps_ok, 1)
            for u in range(8, T * C):
                copy_turned(u)

            for c in range(C):
                act.wait_ge(carry_done, c + 1)
                nc.scalar.copy(carry_sb[:, c * CH:(c + 1) * CH], ps[0:2 * T, C + c, :]).then_inc(carry_sb_ok, 1)
            for c in range(C):
                act.wait_ge(w_bc_done, c + 1)
                nc.scalar.copy(w_bc[:, c * CH:(c + 1) * CH], ps[:, c, :]).then_inc(w_bc_ok, 1)

            def inverse(J, first=False):
                act.wait_ge(num_added, (J + T) * C + C)
                for h in range(2):
                    n = 2 * J + h
                    half = square[:, h * H:(h + 1) * H]
                    if not first:
                        act.wait_ge(att_ok, n - 1)
                    nc.scalar.activation(half, big[:, J, h * H:(h + 1) * H],
                                         ACT.Square).then_inc(squared, 1)
                    act.wait_ge(squared, n + 1)
                    nc.scalar.activation(half, half, ACT.Ln, bias=eps_col[:, 1:2]).then_inc(logged, 1)
                    act.wait_ge(logged, n + 1)
                    nc.scalar.activation(half, half, ACT.Exp, scale=-1.0).then_inc(recip_ok, 1)

            nc.scalar.preload_act_table_set("natural_log_exp_and_others")
            inverse(0, True)
            inverse(1)
            with act.Fori(1, T // 2) as j:
                inverse(2 * j)
                inverse(2 * j + 1)

            for c in range(C):
                act.wait_ge(prod_done, c + 1)
                if c >= 2:
                    act.wait_ge(prod_turned, c - 1)
                nc.scalar.copy(prod_t[:, c % 2, :], ps[:, C + c, :]).then_inc(prod_sb, 1)

        @block.vector
        def _(dve):
            chain = [0]

            def link(ins):
                chain[0] += 1
                ins.then_inc(dve_step, 1)
                dve.wait_ge(dve_step, chain[0])

            def loose(ins):
                chain[0] += 1
                ins.then_inc(dve_step, 1)

            V = nc.vector
            V.memset(eps_col[:, 0:1], EPS).then_inc(var_ok, 1)
            loose(V.memset(eps_col[:, 1:2], TINY))
            dve.wait_ge(ld_x, 16)
            for t in range(T):
                loose(V.bn_stats(stats[:, t, :], x_sb[:, t, :]))
            for t in range(T):
                dve.wait_ge(dve_step, t + 2)
                V.bn_aggr(mean_var[:, t, :], stats[:, t, :]).then_inc(var_ok, 1)
            dve.wait_ge(w_turned, 1)
            V.tensor_copy(w_t, ps[:, 0, 0:P]).then_inc(w_turned_sb, 1)
            V.tensor_copy(a_t[:], ps[:, 1, 0:2]).then_inc(w_turned_sb, 1)
            dve.wait_ge(std_ok, 1)
            link(V.reciprocal(rstd, std))
            for t in range(T):
                V.tensor_scalar(x_sb[:, t, :], x_sb[:, t, :], mean_var[:, t, 0:1], rstd[:, t:t + 1],
                                ALU.subtract, ALU.mult).then_inc(norm_ok, 1)
            dve.wait_ge(wa_done, 1)
            V.tensor_copy(w_aug[:, FO:FA], ps[:, 2, 0:2]).then_inc(wa_sb, 1)
            dve.wait_ge(wa_sb, 1)
            dve.wait_ge(ident_zero, 2)
            V.tensor_scalar(w_rep, ones[:], w_aug[:, FO + 1:FA], None, ALU.mult).then_inc(wa_sb, 1)
            for g in range(C):
                dve.wait_ge(h_turned, g + 1)
                V.tensor_scalar(h_t[:, g * CH:(g + 1) * CH], ps[:, C + g, :], 0.0, None, ALU.max).then_inc(h_sb, 1)
            for b in range(T // 2):
                dve.wait_ge(xw_done, b + 1)
                pair = ps[:, b, :].rearrange("p (k n) -> p k n", k=2)
                V.tensor_copy(table[:, 2 * b:2 * b + 2, 0:FA], pair[:, :, 0:FA]).then_inc(xw_sb, 1)
            dve.wait_ge(xw_sb, T // 2)
            dve.wait_ge(consts, 1)
            V.tensor_tensor(c_diag, ident[:].unsqueeze(1).broadcast_to((P, T, P)),
                            table[:, :, COL_C:COL_C + 1].broadcast_to((P, T, P)), ALU.mult).then_inc(c_diag_ok, 1)
            for c in range(C):
                dve.wait_ge(bc_done, C + c + 1)
                V.tensor_copy(col_bc[:, c * CH:(c + 1) * CH], ps[:, c, :]).then_inc(bc_sb_dve, 1)
            dve.wait_ge(bc_sb_act, C)
            dve.wait_ge(xw_sb, T // 2)
            link(V.tensor_reduce(smax[:], row_bc[:], AX_X, ALU.max))
            V.tensor_scalar(shift[:, 0:1], smax[:], STEEP, None, ALU.mult).then_inc(smax_ok, 1)
            V.tensor_scalar(shift[:, 1:2], smax[:], -STEEP, None, ALU.mult).then_inc(smax_ok, 1)
            V.tensor_copy(s_nat[:], table[:, :, COL_S]).then_inc(smax_ok, 1)
            V.tensor_copy(c_nat[:], table[:, :, COL_C]).then_inc(smax_ok, 1)
            link(V.memset(counts[:], 0.0))
            dve.wait_ge(smax_ok, 4)

            dve.wait_ge(bc_sb_dve, C)
            dve.wait_ge(bc_done, 2 * C)
            dve.wait_ge(tri_ok, 8)
            rank_steps = []
            for t in range(T):
                score = c_nat[:, t:t + 1]
                own = slice(t * P, (t + 1) * P)
                out_to = compared[t % 2]
                if t >= 2:
                    dve.wait_ge(dve_step, rank_steps[t - 2])
                if t:
                    loose(V.tensor_scalar(out_to[:, 0:t * P], col_bc[:, 0:t * P], score, None, ALU.is_le, ALU.add,
                                          accum_out=counts[:, 0, t:t + 1]))
                loose(V.tensor_scalar(out_to[:, t * P:N], col_bc[:, t * P:N], score, None, ALU.is_lt, ALU.add,
                                      accum_out=counts[:, 1, t:t + 1]))
                loose(V.scalar_tensor_tensor(out=tied[:, (t % 2) * P:(t % 2 + 1) * P], in0=col_bc[:, own], scalar=score,
                                             in1=after, op0=ALU.is_equal, op1=ALU.mult,
                                             accum_out=counts[:, 2, t:t + 1]))
                rank_steps.append(chain[0])
            dve.wait_ge(dve_step, chain[0])
            link(V.tensor_tensor(rank[:], counts[:, 0, :], counts[:, 1, :], ALU.add))
            link(V.tensor_tensor(rank[:], rank[:], counts[:, 2, :], ALU.add))
            V.tensor_copy(rank_u[:], rank[:]).then_inc(rank_ok, 1)

            def by_tile(v, n):
                return v.unsqueeze(2).broadcast_to((P, v.shape[1], n))

            def by_block(v, n):
                return v.unsqueeze(1).broadcast_to((P, n, v.shape[1]))

            hit = temp(T, T)
            link(V.tensor_tensor(hit, by_tile(rank[:], T), by_block(iota_tile[:], T), ALU.is_equal))
            link(V.tensor_tensor(hit, hit, by_tile(c_nat[:], T), ALU.mult))
            V.tensor_reduce(bound_in, hit.rearrange("p t b -> p b t"), AX_X, ALU.add).then_inc(bound_in_ok, 1)
            minus_s = temp(T)
            link(V.tensor_scalar(minus_s, s_nat[:], -1.0, None, ALU.mult))
            loose(V.memset(member_ext[:, :, 0:1], 1.0))
            loose(V.memset(member_ext[:, :, T:T + 1], 0.0))
            dve.wait_ge(bound_done, 1)
            link(V.tensor_tensor(member_ext[:, :, 1:T], by_block(ps[:, 0, 1:T], T), by_tile(minus_s, T - 1), ALU.is_le))
            V.tensor_tensor(member, member_ext[:, :, 0:T], member_ext[:, :, 1:T + 1],
                            ALU.subtract).then_inc(weights_ok, 1)
            dve.wait_ge(weights_ok, 1)
            dve.wait_ge(exps_ok, 3)
            link(V.tensor_tensor(gp_nat[:], gp_nat[:], p_nat[:], ALU.mult))
            link(V.tensor_scalar(carry_w[:, :, 0:T], member_ext[:, :, 0:T], -1.0, 1.0, ALU.mult, ALU.add))
            V.tensor_tensor(carry_w[:, :, 0:T], carry_w[:, :, 0:T], by_tile(gp_nat[:], T), ALU.mult).then_inc(weights_ok, 1)
            V.tensor_tensor(carry_w[:, :, T:2 * T], member_ext[:, :, 1:T + 1], by_tile(p_nat[:], T),
                            ALU.mult).then_inc(weights_ok, 1)
            total = totals
            loose(V.memset(total[0][:, 0:PAD, :], 0.0))
            loose(V.memset(total[1][:, 0:PAD, :], 0.0))
            dve.wait_ge(prefix_done, 1)
            link(V.tensor_copy(total[0][:, PAD:, :], ps[:, 2, 0:T * T].rearrange("p (t b) -> p t b", b=T)))
            d, src = 1, 0
            while d < T:
                link(V.tensor_tensor(total[1 - src][:, PAD:, :], total[src][:, PAD:, :],
                                     total[src][:, PAD - d:PAD - d + T, :], ALU.add))
                src, d = 1 - src, 2 * d
            upto = total[src]
            in_block = upto[:, PAD + T - 1, :]
            place_all = hit
            link(V.tensor_tensor(place_all, ps[:, 1, 0:T * T].rearrange("p (t b) -> p t b", b=T),
                                 upto[:, PAD - 1:PAD - 1 + T, :], ALU.add))
            link(V.tensor_tensor(place_all, place_all, member, ALU.mult))
            place = minus_s
            link(V.tensor_reduce(place, place_all, AX_X, ALU.add))
            steps = [temp(PAD + T), temp(PAD + T)]
            loose(V.memset(steps[0][:, 0:PAD], 0.0))
            loose(V.memset(steps[1][:, 0:PAD], 0.0))
            link(V.tensor_tensor(hit, by_tile(in_block, T), by_block(iota_chunk[:], T), ALU.is_gt))
            link(V.tensor_reduce(steps[0][:, PAD:], hit, AX_X, ALU.add))
            link(V.tensor_scalar(steps[0][:, PAD:], steps[0][:, PAD:], 1.0, None, ALU.add))
            own_steps = bound_in
            link(V.tensor_copy(own_steps, steps[0][:, PAD:]))
            d, src = 1, 0
            while d < T:
                link(V.tensor_tensor(steps[1 - src][:, PAD:], steps[src][:, PAD:], steps[src][:, PAD - d:PAD - d + T],
                                     ALU.add))
                src, d = 1 - src, 2 * d
            last_step, first_step = steps[src][:, PAD:], steps[1 - src][:, PAD:]
            link(V.tensor_tensor(first_step, last_step, own_steps, ALU.subtract))
            link(V.tensor_tensor(hit, member, by_block(first_step, T), ALU.mult))
            node_step = temp(T)
            link(V.tensor_reduce(node_step, hit, AX_X, ALU.add))
            link(V.tensor_tensor(hit, by_tile(place, T), by_block(iota_chunk[:], T), ALU.is_ge))
            full = temp(T)
            link(V.tensor_reduce(full, hit, AX_X, ALU.add))
            link(V.tensor_tensor(node_step, node_step, full, ALU.add))
            link(V.scalar_tensor_tensor(out=place, in0=full, scalar=-float(R), in1=place, op0=ALU.mult, op1=ALU.add))
            loose(V.tensor_tensor(pick_row, by_tile(place, P), by_block(iota_row, T), ALU.is_equal))
            link(V.tensor_tensor(in_step, by_tile(node_step, S), by_block(iota_step[:], T), ALU.is_equal))
            for f, v in enumerate((node[:], gp_nat[:], p_nat[:])):
                loose(V.tensor_tensor(pick_step[:, :, f * S:(f + 1) * S], in_step, by_tile(v, S), ALU.mult))
            dve.wait_ge(dve_step, chain[0])
            V.memset(zeros, 0.0).then_inc(pick_ok, 1)
            link(V.tensor_tensor(wide[:, :, 0:T - 1], by_block(last_step[:, 0:T - 1], S), by_tile(iota_step[:], T - 1),
                                 ALU.is_le))
            link(V.tensor_reduce(block_of[:], wide[:, :, 0:T - 1], AX_X, ALU.add))
            link(V.tensor_tensor(wide, by_block(first_step, S), by_tile(iota_step[:], T), ALU.is_equal))
            begins = goes_on
            link(V.tensor_reduce(begins[:], wide, AX_X, ALU.add))
            link(V.tensor_copy(block_int[:], block_of[:]))
            loose(V.tensor_scalar(row_flag[:, 0:1], prow[:], float(R), None, ALU.is_equal))
            link(V.tensor_scalar(row_flag[:, 1:2], prow[:], float(R + 1), None, ALU.is_equal))
            link(V.tensor_tensor(row_flag[:, 2:3], row_flag[:, 0:1], row_flag[:, 1:2], ALU.add))
            link(V.tensor_scalar(row_flag[:, 3:4], row_flag[:, 1:2], float(T), float(N), ALU.mult, ALU.add))
            link(V.tensor_scalar(block_of[:], block_of[:], row_flag[:, 3:4], row_flag[:, 2:3], ALU.add, ALU.mult))
            dve.wait_ge(pick_done, 1)
            link(V.tensor_tensor(block_of[:], block_of[:], ps[:, 3, 0:S], ALU.add))
            loose(V.tensor_copy(slot_idx[:], block_of[:]))
            loose(V.scalar_tensor_tensor(out=slot_gp[:], in0=begins[:], scalar=row_flag[:, 0:1], in1=ps[:, 3, S:2 * S],
                                         op0=ALU.mult, op1=ALU.add))
            link(V.scalar_tensor_tensor(out=slot_p[:], in0=begins[:], scalar=row_flag[:, 1:2],
                                        in1=ps[:, 3, 2 * S:3 * S], op0=ALU.mult, op1=ALU.add))
            V.tensor_scalar(goes_on[:], begins[:], -1.0, 1.0, ALU.mult, ALU.add).then_inc(slots_ok, 1)
            dve.wait_ge(slots_ok, 1)
            dve.wait_ge(table_loaded, 16)
            V.tensor_tensor(diag, ident[:].unsqueeze(1).broadcast_to((P, T, P)),
                            table[:, :, COL_W:FX].broadcast_to((P, T, P)), ALU.mult).then_inc(diag_ok, 1)
            dve.wait_ge(w_bc_ok, C)

            def den(s, k, first=False):
                if not first:
                    dve.wait_ge(num_done, (s - 1) * C)
                J = block_reg(s)
                V.tensor_scalar(den_now[:, k, :], w_bc[:, bass.ds(J * P, P)], slot_gp[:, bass.ds(s, 1)],
                                slot_p[:, bass.ds(s, 1)], ALU.mult, ALU.max).then_inc(den_ok, 1)

            def block_reg(s):
                return V.value_load(block_int[0:1, bass.ds(s, 1)], min_val=0, max_val=T - 1)

            def add(s, c, J):
                dve.wait_ge(num_done, s * C + c + 1)
                part = big[:, J, c * CH:(c + 1) * CH]
                V.scalar_tensor_tensor(out=part, in0=part, scalar=goes_on[:, bass.ds(s, 1)], in1=ps[:, c, :],
                                       op0=ALU.mult, op1=ALU.add).then_inc(num_added, 1)

            def numer(J, h):
                V.tensor_scalar(att_num[:, h * H:(h + 1) * H], row_bc[:, h * H:(h + 1) * H],
                                table[:, J, COL_W:FX], 1.0,
                                ALU.mult, ALU.max).then_inc(numer_ok, 1)

            def att(J, h):
                dve.wait_ge(signed_ok, 2 * J + h + 1)
                dve.wait_ge(recip_ok, 2 * J + h + 1)
                half = big[:, J, h * H:(h + 1) * H]
                V.tensor_tensor(half, att_num[:, h * H:(h + 1) * H], square[:, h * H:(h + 1) * H],
                                ALU.mult).then_inc(att_ok, 1)

            def early_step(s, k, last_adds=True):
                J = block_reg(s)
                for c in range(C):
                    add(s, c, J)
                den(s + 2, k % 2)

            def late_step(s, k, first=False, last=False):
                J = block_reg(s)
                add(s, 0, J)
                add(s, 1, J)
                if not first:
                    att(s - T - 1, 0)
                add(s, 2, J)
                if not first:
                    dve.wait_ge(att_ok, 2 * (s - T - 1) + 1)
                numer(s - T, 0)
                add(s, 3, J)
                if not first:
                    att(s - T - 1, 1)
                    dve.wait_ge(att_ok, 2 * (s - T - 1) + 2)
                numer(s - T, 1)
                if not last:
                    den(s + 2, k % 2)

            den(0, 0, True)
            den(1, 1, True)
            with dve.Fori(0, T // RING) as q:
                for k in range(RING):
                    early_step(q * RING + k, k)
            late_step(T, 0, first=True)
            late_step(T + 1, 1)
            with dve.Fori(0, (T - RING) // RING) as q:
                for k in range(RING):
                    late_step(T + LAG + q * RING + k, (LAG + k) % RING)
            late_step(S - 2, 0, last=True)
            late_step(S - 1, 1, last=True)
            att(T - 1, 0)
            att(T - 1, 1)

            for c in range(C):
                dve.wait_ge(att_used, (T - 1) * C + c + 1)
                V.tensor_copy(sum_t[:, c * CH:(c + 1) * CH], ps[:, C + c, :]).then_inc(sum_t_sb, 1)
            for g in range(C):
                dve.wait_ge(sum_turned, g + 1)
                V.tensor_tensor(att_sum[:, g * G:(g + 1) * G, :], ps[:, g, :].rearrange("p (k f) -> p k f", k=G),
                                by_tile(p_nat[:, g * G:(g + 1) * G], P), ALU.mult).then_inc(sum_sb, 1)
            dve.wait_ge(x_loaded, 16)
            for c in range(C):
                dve.wait_ge(prod_turned, c + 1)
                if c >= 2:
                    dve.wait_ge(stored[c % 2], 16)
                V.tensor_tensor(result[:, c % 2], ps[:, c % 2, :].rearrange("p (k f) -> p k f", k=G),
                                x_again[:, c * G:(c + 1) * G, :], ALU.add).then_inc(res_ok, 1)


_INS = ["x", "adj", "L0_gnn_W", "L0_gnn_a"]


def kernel(**inputs):
    import numpy as _np
    import concourse.bacc as _bacc
    from concourse import mybir as _mybir
    from concourse.bass_utils import run_bass_kernel_spmd as _run

    nc = _bacc.Bacc("TRN2", target_bir_lowering=False, num_devices=1)
    arrays, args = {}, []
    for name in _INS:
        v = _np.ascontiguousarray(inputs[name])
        arrays[f"in_{name}"] = v
        args.append(nc.dram_tensor(f"in_{name}", v.shape, _mybir.dt.from_np(v.dtype), kind="ExternalInput").ap())
    out = nc.dram_tensor("out", inputs["x"].shape, _mybir.dt.float32, kind="ExternalOutput").ap()
    build_gnn(nc, *args, out)
    r = _run(nc, [arrays], core_ids=[0])
    return r.results[0]["out"]
```

```python
from contextlib import ExitStack

import concourse.bass as bass
from concourse import mybir


ALU = mybir.AluOpType
ACT = mybir.ActivationFunctionType
AX_X = mybir.AxisListType.X
F32 = mybir.dt.float32
BF16 = mybir.dt.bfloat16
U32 = mybir.dt.uint32
I32 = mybir.dt.int32

P = 128
SLOPE = 0.01
STEEP = 1.0 - SLOPE
EPS = 1e-5
CH = 512
TINY = 1e-19


def build_gnn(nc, x, adj, w, a, out):
    N, FI = x.shape
    FO = w.shape[1]
    assert FI == P and FO == P and N % (4 * CH) == 0
    T = N // P
    C = N // CH
    G = CH // P
    FA = FO + 2
    COL_C, COL_S, COL_W, FX = FO, FO + 1, FO + 2, FO + 3
    R = P - 2
    S = (N + R * T) // R
    assert S == 2 * T
    LAG = 3
    EARLY = 1
    XW_B = 3
    XW_BANKS = -(-T // XW_B)
    RANK_FROM = 11
    RING = 4
    H = N // 2

    x_rows = x.rearrange("(t p) f -> p t f", p=P)
    out_rows = out.rearrange("(t p) f -> p t f", p=P)
    a_halves = a.rearrange("o (h f) -> (o h) f", h=2)

    with ExitStack() as ctx:
        def sb(name, shape, dt=F32):
            return ctx.enter_context(nc.sbuf_tensor(name, shape, dt))

        def sem(name):
            return ctx.enter_context(nc.semaphore(name))

        adj_t_dram = nc.dram_tensor("adj_t_dram", (N + 2 * T, N), F32, kind="Internal").ap()
        adj_t_rows = adj_t_dram[0:N, :].rearrange("(t p) i -> p t i", p=P)
        adj_t_halves = adj_t_dram.rearrange("k (h i) -> (k h) i", h=2)
        table_dram = nc.dram_tensor("table_dram", (N, FX), F32, kind="Internal").ap()

        ps = ctx.enter_context(nc.psum_tensor("ps", [P, 8, CH], F32))

        big = sb("big", [P, T, N])
        ring = sb("ring", [P, RING, N])
        row_bc = sb("row_bc", [P, N])
        reg_w = sb("reg_w", [P, N])
        reg_sq = sb("reg_sq", [P, N])
        reg_n = sb("reg_n", [P, N])
        table = sb("table", [P, T, FX])

        x_sb = reg_w[:, :].rearrange("p (t f) -> p t f", f=P)
        pick_row = reg_w[:, :].rearrange("p (t r) -> p t r", r=P)
        w_bc = reg_w
        h_t = reg_sq
        compared = [v[:, k * H:(k + 1) * H].bitcast(BF16) for v in (reg_w, reg_sq) for k in range(2)]
        diag = reg_sq[:, :].rearrange("p (t r) -> p t r", r=P)
        square = reg_sq
        col_bc = reg_n
        c_diag = reg_n[:, :].rearrange("p (t r) -> p t r", r=P)
        att_num = reg_n

        used = [0]

        def temp(*shape):
            n = 1
            for d in shape:
                n *= d
            at = used[0]
            used[0] += n
            assert used[0] <= N
            v = reg_n[:, at:at + n]
            if len(shape) == 2:
                v = v.rearrange("p (a b) -> p a b", b=shape[1])
            return v

        ident = sb("ident", [P, P])
        ones = sb("ones", [P, P])
        fold = sb("fold", [P, 2 * T])
        ones_short = sb("ones_short", [P, 2], BF16)
        w_aug = sb("w_aug", [P, FA])
        iota_step = sb("iota_step", [P, S])
        iota_tile = sb("iota_tile", [P, T])
        iota_chunk = sb("iota_chunk", [P, T])
        node = sb("node", [P, T])
        prow = sb("prow", [P, 1])
        row_flag = sb("row_flag", [P, 4])
        a_t = sb("a_t", [P, 2])
        s_nat = sb("s_nat", [P, T])
        c_nat = sb("c_nat", [P, T])
        p_nat = sb("p_nat", [P, T])
        gp_nat = sb("gp_nat", [P, T])
        smax = sb("smax", [P, 1])
        shift = sb("shift", [P, 2])
        eps_col = sb("eps_col", [P, 2])
        counts = sb("counts", [P, 2, T])
        rank = sb("rank", [P, T])
        rank_u = sb("rank_u", [P, T], U32)
        slot_idx = sb("slot_idx", [P, S], U32)
        half_idx = sb("half_idx", [P, 2, EARLY], U32)
        slot_gp = sb("slot_gp", [P, S])
        slot_p = sb("slot_p", [P, S])
        block_of = sb("block_of", [P, S])
        block_int = sb("block_int", [P, S], I32)
        goes_on = sb("goes_on", [P, S])
        den_now = sb("den_now", [P, RING, P])
        xw_now = sb("xw_now", [P, RING, FO])
        before, after, iota_row, w_rep = [xw_now[:, k, :] for k in range(4)]
        bound_in = temp(T)
        member_ext = temp(T, T + 1)
        member = temp(T, T)
        member_flat = member.rearrange("p a b -> p (a b)")
        carry_w = temp(T, 2 * T)
        in_step = reg_sq[:, 0:T * S].rearrange("p (t s) -> p t s", s=S)
        pick_step = reg_sq[:, T * S:4 * T * S].rearrange("p (t n) -> p t n", n=3 * S)
        w_t = den_now[:, 0, :]
        a_in = den_now[0:2, 1, :]
        zeros = den_now[:, 2:4, :].rearrange("p k n -> p (k n)").bitcast(BF16)
        stats = row_bc[:, 0:6 * T].rearrange("p (t n) -> p t n", n=6)
        mean_var = row_bc[:, 6 * T:8 * T].rearrange("p (t n) -> p t n", n=2)
        std = row_bc[:, 8 * T:9 * T]
        rstd = row_bc[:, 9 * T:10 * T]
        PAD = T // 2
        TOTAL = (PAD + T) * T
        totals = [ring[:, 3, k * TOTAL:(k + 1) * TOTAL].rearrange("p (t b) -> p t b", b=T) for k in range(2)]
        wide = ring[:, 3, 2 * TOTAL:2 * TOTAL + S * T].rearrange("p (s b) -> p s b", b=T)
        tied = den_now[:, 0, :].bitcast(BF16)
        carry_parts = ring[:, 0, :]
        carry_sb = ring[0:2 * T, 1, :]

        sum_t = ring[:, 0, :]
        x_again = ring[:, 1, :].rearrange("p (t f) -> p t f", f=P)
        att_sum = ring[:, 2, :].rearrange("p (t f) -> p t f", f=P)
        prod_t = ring[:, 3, 0:2 * CH].rearrange("p (s n) -> p s n", s=2)
        result = ring[:, 3, 2 * CH:4 * CH].rearrange("p (s g f) -> p s g f", s=2, f=P)

        names = """ld_x ld_w ld_a ident_zero consts tri_ok zeros_ok w_turned w_turned_sb wa_done wa_sb std_ok var_ok
            norm_ok h_turned h_sb xw_done xw_sb c_diag_ok bc_done bc_sb_dve bc_sb_act adj_turned adj_sb dve_step
            compared_ok later_counted smax_ok exps_ok w_in_table rank_ok table_stored table_loaded bound_in_ok
            bound_done prefix_done weights_ok fold_ok carry_done carry_parts_ok fold_done carry_sb_ok carry_stored
            pick_ok pick_done slots_ok diag_ok w_bc_done w_bc_ok den_ok num_done num_added squared logged recip_ok
            numer_ok signed_ok att_ok xw_now_ok att_used x_loaded sum_t_sb sum_turned sum_sb prod_done prod_sb
            prod_turned res_ok""".split()
        sems = {n: sem(n) for n in names}
        (ld_x, ld_w, ld_a, ident_zero, consts, tri_ok, zeros_ok, w_turned, w_turned_sb, wa_done, wa_sb, std_ok,
         var_ok, norm_ok, h_turned, h_sb, xw_done, xw_sb, c_diag_ok, bc_done, bc_sb_dve, bc_sb_act, adj_turned,
         adj_sb, dve_step, compared_ok, later_counted, smax_ok, exps_ok, w_in_table, rank_ok, table_stored,
         table_loaded, bound_in_ok, bound_done, prefix_done, weights_ok, fold_ok, carry_done, carry_parts_ok,
         fold_done, carry_sb_ok, carry_stored, pick_ok, pick_done, slots_ok, diag_ok, w_bc_done, w_bc_ok, den_ok,
         num_done, num_added, squared, logged, recip_ok, numer_ok, signed_ok, att_ok, xw_now_ok, att_used, x_loaded,
         sum_t_sb, sum_turned, sum_sb, prod_done, prod_sb, prod_turned, res_ok) = [sems[n] for n in names]
        ld_adj = [sem(f"ld_adj{s}") for s in range(RING)]
        adj_t_stored = [sem("adj_t_stored0"), sem("adj_t_stored1")]
        gathered = [sem(f"gathered{s}") for s in range(RING)]
        gathered_half = [sem(f"gathered_half{s}") for s in range(EARLY)]
        reloaded = [sem(f"reloaded{t}") for t in range(T)]
        stored = [sem("stored0"), sem("stored1")]
        PIECE_T = 2
        PIECES = 2 * T // PIECE_T

        def early(n):
            h, s = n // (EARLY * C // 2), n // (C // 2) % EARLY
            return h, s, h * (C // 2) + n % (C // 2)

        block = ctx.enter_context(nc.Block())

        @block.sync
        def _(sp):
            sp.dma_start(x_sb, x_rows).then_inc(ld_x, 16)
            sp.dma_start(w_aug[:, 0:FO], w).then_inc(ld_w, 16)
            sp.dma_start(a_in, a_halves).then_inc(ld_a, 16)
            for r in range(T):
                s = r % RING
                if r >= RING:
                    sp.wait_ge(adj_turned, (r - RING + 1) * C)
                sp.dma_start(ring[:, s, :], adj[r * P:(r + 1) * P, :]).then_inc(ld_adj[s], 16)
            for k in range(PIECES):
                half, t = k // (PIECES // 2), k % (PIECES // 2) * PIECE_T
                if t == 0:
                    sp.wait_ge(adj_sb, (half + 1) * T * C // 2)
                if k >= 2:
                    sp.wait_ge(adj_t_stored[k % 2], 16 * (k // 2))
                sp.dma_start(adj_t_rows[:, t:t + PIECE_T, half * H:(half + 1) * H],
                             big[:, t:t + PIECE_T, half * H:(half + 1) * H]).then_inc(adj_t_stored[k % 2], 16)
            for t in range(T):
                sp.wait_ge(att_used, t * C + C)
                sp.dma_start(big[:, t, :], adj_t_dram[t * P:(t + 1) * P, :]).then_inc(reloaded[t], 16)
            sp.wait_ge(num_done, S * C)
            sp.dma_start(x_again, x_rows).then_inc(x_loaded, 16)
            for c in range(C):
                sp.wait_ge(res_ok, c + 1)
                sp.dma_start(out_rows[:, c * G:(c + 1) * G, :], result[:, c % 2]).then_inc(stored[c % 2], 16)
            for s in range(2):
                sp.wait_ge(stored[s], 16 * C // 2)

        @block.gpsimd
        def _(pool):
            nc.gpsimd.memset(ident[:], 0.0).then_inc(ident_zero, 1)
            nc.gpsimd.memset(ones[:], 1.0).then_inc(ident_zero, 1)
            pool.wait_ge(ident_zero, 2)
            nc.gpsimd.affine_select(out=ident[:], in_=ident[:], compare_op=ALU.not_equal, fill=1.0, base=0,
                                    pattern=[[-1, P]], channel_multiplier=1).then_inc(consts, 1)
            nc.gpsimd.affine_select(out=before, in_=ones[:], compare_op=ALU.is_gt, fill=0.0, base=0,
                                    pattern=[[1, P]], channel_multiplier=-1).then_inc(tri_ok, 1)
            nc.gpsimd.affine_select(out=after, in_=ones[:], compare_op=ALU.is_gt, fill=0.0, base=0,
                                    pattern=[[-1, P]], channel_multiplier=1).then_inc(tri_ok, 1)
            for t, base, step, mult in ((iota_row, 0, 1, 0), (iota_step, 0, 1, 0), (iota_tile, 0, P, 0),
                                        (iota_chunk, R, R, 0), (node, 0, P, 1), (prow, 0, 0, 1)):
                nc.gpsimd.iota(t[:, :], pattern=[[step, t.shape[1]]], base=base, channel_multiplier=mult,
                               allow_small_or_imprecise_dtypes=True).then_inc(tri_ok, 1)
            pool.wait_ge(rank_ok, 1)
            pool.wait_ge(w_in_table, 1)
            pool.wait_ge(xw_sb, XW_BANKS)
            for t in range(T):
                nc.gpsimd.indirect_dma_start(
                    out=table_dram, out_offset=bass.IndirectOffsetOnAxis(ap=rank_u[:, t:t + 1], axis=0),
                    in_=table[:, t, :], in_offset=None).then_inc(table_stored, 16)
            pool.wait_ge(table_stored, 16 * T)
            pool.dma_start(table[:], table_dram.rearrange("(t p) f -> p t f", p=P)).then_inc(table_loaded, 16)

            def gather(s):
                if s >= RING:
                    pool.wait_ge(num_done, (s - RING + 1) * C if s >= RING + EARLY else (EARLY + s - RING + 1) * C // 2)
                nc.gpsimd.indirect_dma_start(
                    out=ring[:, s % RING, :], out_offset=None, in_=adj_t_dram,
                    in_offset=bass.IndirectOffsetOnAxis(ap=slot_idx[:, s:s + 1], axis=0)).then_inc(
                        gathered[s % RING], 16)

            def gather_half(s, h):
                nc.gpsimd.indirect_dma_start(
                    out=ring[:, s, h * H:(h + 1) * H], out_offset=None, in_=adj_t_halves,
                    in_offset=bass.IndirectOffsetOnAxis(ap=half_idx[:, h, s:s + 1], axis=0)).then_inc(
                        gathered[s] if h else gathered_half[s], 16)

            def numerator(J):
                pool.wait_ge(num_added, (J + T) * C + C)
                for h in range(2):
                    pool.wait_ge(numer_ok, 2 * J + h + 1)
                    nc.gpsimd.tensor_tensor(att_num[:, h * H:(h + 1) * H], att_num[:, h * H:(h + 1) * H],
                                            big[:, J, h * H:(h + 1) * H],
                                            ALU.mult).then_inc(signed_ok, 1)

            def xw_copy(J):
                if J >= RING:
                    pool.wait_ge(att_used, (J - RING) * C + C)
                nc.gpsimd.tensor_copy(xw_now[:, J % RING, :], table[:, J, 0:FO]).then_inc(xw_now_ok, 1)

            pool.wait_ge(slots_ok, 1)
            pool.wait_ge(carry_stored, 16)
            for h in range(2):
                for k in range(2):
                    pool.wait_ge(adj_t_stored[k], 16 * (h + 1) * PIECES // 4)
                for s in range(EARLY):
                    gather_half(s, h)
            for s in range(EARLY, RING):
                gather(s)
            pool.wait_ge(table_loaded, 16)
            for J in range(RING):
                xw_copy(J)
            for s in range(RING, T + RING):
                gather(s)
            for J in range(T):
                if J + T + RING < S:
                    gather(J + T + RING)
                if J >= RING:
                    xw_copy(J)
                numerator(J)

        @block.tensor
        def _(pe):
            def turn_group(r, g):
                if g == 0:
                    pe.wait_ge(ld_adj[r % RING], (r // RING + 1) * 16)
                if r:
                    pe.wait_ge(adj_sb, (r - 1) * C + g + 1)
                for k in range(G):
                    t = g * G + k
                    last = nc.tensor.transpose(ps[:, C + g, k * P:(k + 1) * P],
                                               ring[:, r % RING, t * P:(t + 1) * P], ident[:])
                last.then_inc(adj_turned, 1)

            def turn_adj(r):
                for g in range(C):
                    turn_group(r, g)

            def keep_warm(bank, n):
                for _ in range(n):
                    nc.tensor.matmul(ps[:, bank, :], zeros[:, 0:P], zeros[:], start=True, stop=True)

            pe.wait_ge(zeros_ok, 2)
            keep_warm(3, 11)
            pe.wait_ge(consts, 1)
            pe.wait_ge(ld_w, 16)
            pe.wait_ge(ld_a, 16)
            nc.tensor.transpose(ps[:, 0, 0:P], w_aug[:, 0:FO], ident[:])
            nc.tensor.transpose(ps[:, 1, 0:2], a_in, ident[0:2, 0:2]).then_inc(w_turned, 1)
            keep_warm(3, 7)
            turn_adj(0)
            pe.wait_ge(w_turned_sb, 2)
            nc.tensor.matmul(ps[:, 3, 0:2], w_t, a_t[:], start=True, stop=True).then_inc(wa_done, 1)
            for g in range(C):
                if g == 3:
                    pe.wait_ge(wa_sb, 1)
                for k in range(G):
                    t = g * G + k
                    pe.wait_ge(norm_ok, t + 1)
                    last = nc.tensor.transpose(ps[:, g, k * P:(k + 1) * P], x_sb[:, t, :], ident[:])
                last.then_inc(h_turned, 1)
                turn_group(1, g)
            turn_adj(2)
            pe.wait_ge(wa_sb, 1)
            pe.wait_ge(h_sb, C)
            for t in range(T):
                b = t // XW_B
                if b >= C and t % XW_B == 0:
                    pe.wait_ge(xw_sb, b - C + 1)
                last = nc.tensor.matmul(ps[:, b % C, t % XW_B * FA:(t % XW_B + 1) * FA], h_t[:, t * P:(t + 1) * P],
                                        w_aug[:], start=True, stop=True, skip_group_check=True)
                if t % XW_B == XW_B - 1 or t == T - 1:
                    last.then_inc(xw_done, 1)
            turn_adj(3)

            def row_scores(c):
                pe.wait_ge(xw_sb, c + 3)
                nc.tensor.matmul(ps[:, (c + 2) % C, :], w_rep, h_t[:, c * CH:(c + 1) * CH], start=True,
                                 stop=True).then_inc(bc_done, 1)

            def col_scores(c):
                pe.wait_ge(c_diag_ok, c + 1)
                pe.wait_ge(bc_sb_act, c + 1)
                nc.tensor.matmul(ps[:, (c + 2) % C, :], ones[:], c_diag[:, c * G:(c + 1) * G, :], start=True,
                                 stop=True).then_inc(bc_done, 1)

            pe.wait_ge(wa_sb, 2)
            row_scores(0)
            row_scores(1)
            turn_adj(4)
            row_scores(2)
            row_scores(3)
            turn_adj(5)
            turn_adj(6)
            col_scores(0)
            col_scores(1)
            turn_adj(7)
            col_scores(2)
            col_scores(3)

            def count_later(t):
                pe.wait_ge(compared_ok, t + 1)
                for b in range(t + 1, T):
                    last = nc.tensor.matmul(ps[:, 0, b:b + 1], compared[t % 4][:, b * P:(b + 1) * P],
                                            ones_short[:, 0:1], start=False, stop=False, skip_group_check=True)
                last.then_inc(later_counted, 1)

            pe.wait_ge(bc_sb_dve, C)
            nc.tensor.matmul(ps[:, 0, 0:T], zeros[:, 0:P], zeros[:, 0:T], start=True, stop=False,
                             skip_group_check=True)
            for r in range(8, T):
                turn_adj(r)
                if r >= RANK_FROM:
                    count_later(r - RANK_FROM)
            for t in range(T - RANK_FROM, T - 1):
                count_later(t)

            pe.wait_ge(tri_ok, 2)
            pe.wait_ge(bound_in_ok, 1)
            nc.tensor.matmul(ps[:, 1, 0:T], ones[:], bound_in, start=True, stop=True).then_inc(bound_done, 1)
            pe.wait_ge(weights_ok, 1)
            nc.tensor.matmul(ps[:, 2, 0:T * T], before, member_flat, start=True, stop=True)
            nc.tensor.matmul(ps[:, 3, 0:T * T], ones[:], member_flat, start=True, stop=True).then_inc(prefix_done, 1)

            def carries(c):
                for t in range(T):
                    q = t % 4 * 2 * T
                    last = nc.tensor.matmul(ps[q:q + 2 * T, C + c, :], carry_w[:, t, :],
                                            big[:, t, c * CH:(c + 1) * CH],
                                            start=(t < 4), stop=(t >= T - 4))
                last.then_inc(carry_done, 1)

            pe.wait_ge(adj_sb, T * C)
            pe.wait_ge(weights_ok, 3)
            for c in range(C - 1):
                carries(c)
            pe.wait_ge(pick_ok, 3)
            for t in range(T):
                last = nc.tensor.matmul(ps[:, 3, 0:3 * S], pick_row[:, t, :], pick_step[:, t, :],
                                        start=(t == 0), stop=(t == T - 1))
            last.then_inc(pick_done, 1)
            carries(C - 1)
            pe.wait_ge(fold_ok, 1)
            for c in range(C):
                pe.wait_ge(carry_parts_ok, c + 1)
                nc.tensor.matmul(ps[0:2 * T, C + c, :], fold[:], carry_parts[:, c * CH:(c + 1) * CH], start=True,
                                 stop=True).then_inc(fold_done, 1)
            pe.wait_ge(slots_ok, 1)
            for c in range(C):
                pe.wait_ge(diag_ok, c + 1)
                nc.tensor.matmul(ps[:, c, :], ones[:], diag[:, c * G:(c + 1) * G, :], start=True,
                                 stop=True).then_inc(w_bc_done, 1)
            pe.wait_ge(carry_sb_ok, C)
            for c in range(C):
                last = nc.tensor.matmul(ps[:, C + c, :], zeros[:, 0:P], zeros[:], start=True, stop=False,
                                        skip_group_check=True)
            last.then_inc(w_bc_done, 1)
            pe.wait_ge(w_bc_ok, C)

            def slots(s, k, c):
                if c == 0:
                    pe.wait_ge(den_ok, s + 1)
                    pe.wait_ge(gathered[k], (s - k) * (16 // RING) + 16)
                pe.wait_ge(num_added, s * C + c - C + 1)
                nc.tensor.matmul(ps[:, c, :], den_now[:, k, :], ring[:, k, c * CH:(c + 1) * CH],
                                 start=True, stop=True).then_inc(num_done, 1)

            def early_slots(n):
                h, s, c = early(n)
                if c % 2 == 0:
                    pe.wait_ge(den_ok, s + 1)
                    pe.wait_ge(gathered[s] if h else gathered_half[s], 16)
                if n >= C:
                    pe.wait_ge(num_added, n - C + 1)
                nc.tensor.matmul(ps[:, n % C, :], den_now[:, s, :], ring[:, s, c * CH:(c + 1) * CH],
                                 start=True, stop=True).then_inc(num_done, 1)

            def product(J, s, c):
                if c == 0:
                    pe.wait_ge(xw_now_ok, J + 1)
                    pe.wait_ge(att_ok, 2 * J + 1)
                if c == C // 2:
                    pe.wait_ge(att_ok, 2 * J + 2)
                nc.tensor.matmul(ps[:, C + c, :], xw_now[:, s, :],
                                 big[:, J, c * CH:(c + 1) * CH],
                                 start=False, stop=False, skip_group_check=True).then_inc(att_used, 1)

            for n in range(EARLY * C):
                early_slots(n)
            for s in range(EARLY, RING):
                for c in range(C):
                    slots(s, s, c)
            with pe.Fori(1, T // RING) as q:
                for k in range(RING):
                    for c in range(C):
                        slots(q * RING + k, k, c)
            for s in range(T, T + LAG):
                for c in range(C):
                    slots(s, s % RING, c)
            with pe.Fori(0, (T - RING) // RING) as q:
                for k in range(RING):
                    for c in range(C):
                        slots(T + LAG + q * RING + k, (LAG + k) % RING, c)
                        product(q * RING + k, k, c)
            for s in range(S - RING + LAG, S):
                for c in range(C):
                    slots(s, s % RING, c)
                    product(s - T - LAG, (s - T - LAG) % RING, c)
            for J in range(T - LAG, T):
                for c in range(C):
                    product(J, J % RING, c)

            for g in range(C):
                pe.wait_ge(sum_t_sb, g + 1)
                for k in range(G):
                    t = g * G + k
                    last = nc.tensor.transpose(ps[:, g, k * P:(k + 1) * P], sum_t[:, t * P:(t + 1) * P], ident[:])
                last.then_inc(sum_turned, 1)
            def turn_product(c):
                pe.wait_ge(prod_sb, c + 1)
                if c >= 2:
                    pe.wait_ge(res_ok, c - 1)
                for k in range(G):
                    last = nc.tensor.transpose(ps[:, c % 2, k * P:(k + 1) * P], prod_t[:, c % 2, k * P:(k + 1) * P],
                                               ident[:])
                last.then_inc(prod_turned, 1)

            for c in range(C):
                for t in range(T):
                    if c == 0:
                        pe.wait_ge(sum_sb, t // G + 1)
                        pe.wait_ge(reloaded[t], 16)
                    last = nc.tensor.matmul(ps[:, C + c, :], att_sum[:, t, :], big[:, t, c * CH:(c + 1) * CH],
                                            start=(t == 0), stop=(t == T - 1))
                last.then_inc(prod_done, 1)
                if c:
                    turn_product(c - 1)
            turn_product(C - 1)

        @block.scalar
        def _(act):
            nc.scalar.preload_act_table_set("sqrt_and_others")

            def copy_turned(r):
                for g in range(C):
                    act.wait_ge(adj_turned, r * C + g + 1)
                    nc.scalar.copy(big[:, g * G:(g + 1) * G, r * P:(r + 1) * P],
                                   ps[:, C + g, :].rearrange("p (k i) -> p k i", k=G)).then_inc(adj_sb, 1)

            act.wait_ge(var_ok, T + 1)
            nc.scalar.activation(std, mean_var[:, :, 1], ACT.Sqrt, bias=eps_col[:, 0:1]).then_inc(std_ok, 1)
            for r in range(4):
                copy_turned(r)

            def copy_scores(c):
                act.wait_ge(bc_done, c + 1)
                nc.scalar.copy(row_bc[:, c * CH:(c + 1) * CH], ps[:, (c + 2) % C, :]).then_inc(bc_sb_act, 1)

            copy_scores(0)
            copy_scores(1)
            copy_turned(4)
            copy_scores(2)
            copy_scores(3)
            for r in range(5, T):
                copy_turned(r)
                if r == RANK_FROM - 2:
                    act.wait_ge(smax_ok, 4)
                    nc.scalar.activation(p_nat[:], s_nat[:], ACT.Exp, scale=SLOPE).then_inc(exps_ok, 1)
                    nc.scalar.activation(gp_nat[:], s_nat[:], ACT.Exp, scale=STEEP,
                                         bias=shift[:, 1:2]).then_inc(exps_ok, 1)
                    nc.scalar.activation(table[:, :, COL_W], c_nat[:], ACT.Exp, scale=STEEP,
                                         bias=shift[:, 0:1]).then_inc(w_in_table, 1)
            nc.scalar.activation(row_bc[:], row_bc[:], ACT.Exp, scale=STEEP, bias=shift[:, 1:2]).then_inc(exps_ok, 1)

            for c in range(C):
                act.wait_ge(carry_done, c + 1)
                nc.scalar.copy(carry_parts[:, c * CH:(c + 1) * CH], ps[:, C + c, :]).then_inc(carry_parts_ok, 1)
            for c in range(C):
                act.wait_ge(fold_done, c + 1)
                nc.scalar.copy(carry_sb[:, c * CH:(c + 1) * CH], ps[0:2 * T, C + c, :]).then_inc(carry_sb_ok, 1)
            act.wait_ge(carry_sb_ok, C)
            act.dma_start(adj_t_dram[N:N + 2 * T, :], carry_sb).then_inc(carry_stored, 16)
            for c in range(C):
                act.wait_ge(w_bc_done, c + 1)
                nc.scalar.copy(w_bc[:, c * CH:(c + 1) * CH], ps[:, c, :]).then_inc(w_bc_ok, 1)

            def inverse(J, first=False):
                act.wait_ge(num_added, (J + T) * C + C)
                for h in range(2):
                    n = 2 * J + h
                    half = square[:, h * H:(h + 1) * H]
                    if not first:
                        act.wait_ge(att_ok, n - 1)
                    nc.scalar.activation(half, big[:, J, h * H:(h + 1) * H],
                                         ACT.Square).then_inc(squared, 1)
                    act.wait_ge(squared, n + 1)
                    nc.scalar.activation(half, half, ACT.Ln, bias=eps_col[:, 1:2]).then_inc(logged, 1)
                    act.wait_ge(logged, n + 1)
                    nc.scalar.activation(half, half, ACT.Exp, scale=-1.0).then_inc(recip_ok, 1)

            nc.scalar.preload_act_table_set("natural_log_exp_and_others")
            inverse(0, True)
            inverse(1)
            with act.Fori(1, T // 2) as j:
                inverse(2 * j)
                inverse(2 * j + 1)

            for c in range(C):
                act.wait_ge(prod_done, c + 1)
                if c >= 2:
                    act.wait_ge(prod_turned, c - 1)
                nc.scalar.copy(prod_t[:, c % 2, :], ps[:, C + c, :]).then_inc(prod_sb, 1)

        @block.vector
        def _(dve):
            chain = [0]

            def link(ins):
                chain[0] += 1
                ins.then_inc(dve_step, 1)
                dve.wait_ge(dve_step, chain[0])

            def loose(ins):
                chain[0] += 1
                ins.then_inc(dve_step, 1)

            V = nc.vector
            V.memset(zeros[:], 0.0).then_inc(zeros_ok, 1)
            V.memset(ones_short[:], 1.0).then_inc(zeros_ok, 1)
            V.memset(eps_col[:, 0:1], EPS).then_inc(var_ok, 1)
            loose(V.memset(eps_col[:, 1:2], TINY))
            dve.wait_ge(ld_x, 16)
            for t in range(T):
                loose(V.bn_stats(stats[:, t, :], x_sb[:, t, :]))
            for t in range(T):
                dve.wait_ge(dve_step, t + 2)
                V.bn_aggr(mean_var[:, t, :], stats[:, t, :]).then_inc(var_ok, 1)
            dve.wait_ge(w_turned, 1)
            V.tensor_copy(w_t, ps[:, 0, 0:P]).then_inc(w_turned_sb, 1)
            V.tensor_copy(a_t[:], ps[:, 1, 0:2]).then_inc(w_turned_sb, 1)
            dve.wait_ge(std_ok, 1)
            link(V.reciprocal(rstd, std))
            for t in range(T):
                V.tensor_scalar(x_sb[:, t, :], x_sb[:, t, :], mean_var[:, t, 0:1], rstd[:, t:t + 1],
                                ALU.subtract, ALU.mult).then_inc(norm_ok, 1)
                if t == T // 2:
                    dve.wait_ge(wa_done, 1)
                    V.tensor_copy(w_aug[:, FO:FA], ps[:, 3, 0:2]).then_inc(wa_sb, 1)
            dve.wait_ge(wa_sb, 1)
            dve.wait_ge(ident_zero, 2)
            V.tensor_scalar(w_rep, ones[:], w_aug[:, FO + 1:FA], None, ALU.mult).then_inc(wa_sb, 1)
            for g in range(C):
                dve.wait_ge(h_turned, g + 1)
                V.tensor_scalar(h_t[:, g * CH:(g + 1) * CH], ps[:, g, :], 0.0, None, ALU.max).then_inc(h_sb, 1)
            for b in range(XW_BANKS):
                dve.wait_ge(xw_done, b + 1)
                n = min(XW_B, T - b * XW_B)
                V.tensor_copy(table[:, b * XW_B:b * XW_B + n, 0:FA],
                              ps[:, b % C, 0:n * FA].rearrange("p (k n) -> p k n", k=n)).then_inc(xw_sb, 1)
            dve.wait_ge(xw_sb, XW_BANKS)
            dve.wait_ge(consts, 1)
            for c in range(C):
                V.tensor_tensor(c_diag[:, c * G:(c + 1) * G, :], ident[:].unsqueeze(1).broadcast_to((P, G, P)),
                                table[:, c * G:(c + 1) * G, COL_C:COL_C + 1].broadcast_to((P, G, P)),
                                ALU.mult).then_inc(c_diag_ok, 1)
            for c in range(C):
                dve.wait_ge(bc_done, C + c + 1)
                V.tensor_copy(col_bc[:, c * CH:(c + 1) * CH], ps[:, (c + 2) % C, :]).then_inc(bc_sb_dve, 1)
            dve.wait_ge(bc_sb_act, C)
            link(V.tensor_reduce(smax[:], row_bc[:], AX_X, ALU.max))
            V.tensor_scalar(shift[:, 0:1], smax[:], STEEP, None, ALU.mult).then_inc(smax_ok, 1)
            V.tensor_scalar(shift[:, 1:2], smax[:], -STEEP, None, ALU.mult).then_inc(smax_ok, 1)
            V.tensor_copy(s_nat[:], table[:, :, COL_S]).then_inc(smax_ok, 1)
            V.tensor_copy(c_nat[:], table[:, :, COL_C]).then_inc(smax_ok, 1)
            link(V.memset(counts[:], 0.0))
            dve.wait_ge(smax_ok, 4)

            dve.wait_ge(bc_sb_dve, C)
            dve.wait_ge(bc_done, 2 * C)
            dve.wait_ge(tri_ok, 8)
            rank_steps = []
            for t in range(T):
                score = c_nat[:, t:t + 1]
                own = slice(t * P, (t + 1) * P)
                out_to = compared[t % 4]
                if t >= 4:
                    dve.wait_ge(later_counted, t - 3)
                V.tensor_scalar(out_to[:, t * P:N], col_bc[:, t * P:N], score, None, ALU.is_lt, ALU.add,
                                accum_out=counts[:, 0, t:t + 1]).then_inc(compared_ok, 1)
                if t >= 2:
                    dve.wait_ge(dve_step, rank_steps[t - 2])
                loose(V.scalar_tensor_tensor(out=tied[:, (t % 2) * P:(t % 2 + 1) * P], in0=col_bc[:, own], scalar=score,
                                             in1=after, op0=ALU.is_equal, op1=ALU.mult,
                                             accum_out=counts[:, 1, t:t + 1]))
                rank_steps.append(chain[0])
            dve.wait_ge(compared_ok, T)
            dve.wait_ge(later_counted, T - 1)
            dve.wait_ge(dve_step, chain[0])
            link(V.tensor_tensor(rank[:], counts[:, 0, :], counts[:, 1, :], ALU.add))
            link(V.tensor_tensor(rank[:], rank[:], iota_tile[:], ALU.add))
            link(V.tensor_tensor(rank[:], rank[:], ps[:, 0, 0:T], ALU.subtract))
            V.tensor_copy(rank_u[:], rank[:]).then_inc(rank_ok, 1)

            def by_tile(v, n):
                return v.unsqueeze(2).broadcast_to((P, v.shape[1], n))

            def by_block(v, n):
                return v.unsqueeze(1).broadcast_to((P, n, v.shape[1]))

            hit = temp(T, T)
            link(V.tensor_tensor(hit, by_tile(rank[:], T), by_block(iota_tile[:], T), ALU.is_equal))
            link(V.tensor_tensor(hit, hit, by_tile(c_nat[:], T), ALU.mult))
            V.tensor_reduce(bound_in, hit.rearrange("p t b -> p b t"), AX_X, ALU.add).then_inc(bound_in_ok, 1)
            minus_s = temp(T)
            link(V.tensor_scalar(minus_s, s_nat[:], -1.0, None, ALU.mult))
            loose(V.memset(member_ext[:, :, 0:1], 1.0))
            loose(V.memset(member_ext[:, :, T:T + 1], 0.0))
            dve.wait_ge(bound_done, 1)
            link(V.tensor_tensor(member_ext[:, :, 1:T], by_block(ps[:, 1, 1:T], T), by_tile(minus_s, T - 1), ALU.is_le))
            V.tensor_tensor(member, member_ext[:, :, 0:T], member_ext[:, :, 1:T + 1],
                            ALU.subtract).then_inc(weights_ok, 1)
            dve.wait_ge(weights_ok, 1)
            V.tensor_reduce(fold[:], ident[:].rearrange("p (q m) -> p m q", q=4), AX_X, ALU.add).then_inc(fold_ok, 1)
            dve.wait_ge(exps_ok, 3)
            link(V.tensor_tensor(gp_nat[:], gp_nat[:], p_nat[:], ALU.mult))
            link(V.tensor_scalar(carry_w[:, :, 0:T], member_ext[:, :, 0:T], -1.0, 1.0, ALU.mult, ALU.add))
            V.tensor_tensor(carry_w[:, :, 0:T], carry_w[:, :, 0:T], by_tile(gp_nat[:], T),
                            ALU.mult).then_inc(weights_ok, 1)
            V.tensor_tensor(carry_w[:, :, T:2 * T], member_ext[:, :, 1:T + 1], by_tile(p_nat[:], T),
                            ALU.mult).then_inc(weights_ok, 1)
            total = totals
            dve.wait_ge(prefix_done, 1)
            loose(V.memset(total[0][:, 0:PAD, :], 0.0))
            loose(V.memset(total[1][:, 0:PAD, :], 0.0))
            link(V.tensor_copy(total[0][:, PAD:, :], ps[:, 3, 0:T * T].rearrange("p (t b) -> p t b", b=T)))
            d, src = 1, 0
            while d < T:
                link(V.tensor_tensor(total[1 - src][:, PAD:, :], total[src][:, PAD:, :],
                                     total[src][:, PAD - d:PAD - d + T, :], ALU.add))
                src, d = 1 - src, 2 * d
            upto = total[src]
            in_block = upto[:, PAD + T - 1, :]
            place_all = hit
            link(V.tensor_tensor(place_all, ps[:, 2, 0:T * T].rearrange("p (t b) -> p t b", b=T),
                                 upto[:, PAD - 1:PAD - 1 + T, :], ALU.add))
            link(V.tensor_tensor(place_all, place_all, member, ALU.mult))
            place = minus_s
            link(V.tensor_reduce(place, place_all, AX_X, ALU.add))
            steps = [temp(PAD + T), temp(PAD + T)]
            loose(V.memset(steps[0][:, 0:PAD], 0.0))
            loose(V.memset(steps[1][:, 0:PAD], 0.0))
            link(V.tensor_tensor(hit, by_tile(in_block, T), by_block(iota_chunk[:], T), ALU.is_gt))
            link(V.tensor_reduce(steps[0][:, PAD:], hit, AX_X, ALU.add))
            link(V.tensor_scalar(steps[0][:, PAD:], steps[0][:, PAD:], 1.0, None, ALU.add))
            own_steps = bound_in
            link(V.tensor_copy(own_steps, steps[0][:, PAD:]))
            d, src = 1, 0
            while d < T:
                link(V.tensor_tensor(steps[1 - src][:, PAD:], steps[src][:, PAD:], steps[src][:, PAD - d:PAD - d + T],
                                     ALU.add))
                src, d = 1 - src, 2 * d
            last_step, first_step = steps[src][:, PAD:], steps[1 - src][:, PAD:]
            link(V.tensor_tensor(first_step, last_step, own_steps, ALU.subtract))
            link(V.tensor_tensor(hit, member, by_block(first_step, T), ALU.mult))
            node_step = temp(T)
            link(V.tensor_reduce(node_step, hit, AX_X, ALU.add))
            link(V.tensor_tensor(hit, by_tile(place, T), by_block(iota_chunk[:], T), ALU.is_ge))
            full = temp(T)
            link(V.tensor_reduce(full, hit, AX_X, ALU.add))
            link(V.tensor_tensor(node_step, node_step, full, ALU.add))
            link(V.scalar_tensor_tensor(out=place, in0=full, scalar=-float(R), in1=place, op0=ALU.mult, op1=ALU.add))
            loose(V.tensor_tensor(pick_row, by_tile(place, P), by_block(iota_row, T), ALU.is_equal))
            link(V.tensor_tensor(in_step, by_tile(node_step, S), by_block(iota_step[:], T), ALU.is_equal))
            for f, v in enumerate((node[:], gp_nat[:], p_nat[:])):
                V.tensor_tensor(pick_step[:, :, f * S:(f + 1) * S], in_step, by_tile(v, S),
                                ALU.mult).then_inc(pick_ok, 1)
            link(V.tensor_tensor(wide[:, :, 0:T - 1], by_block(last_step[:, 0:T - 1], S), by_tile(iota_step[:], T - 1),
                                 ALU.is_le))
            link(V.tensor_reduce(block_of[:], wide[:, :, 0:T - 1], AX_X, ALU.add))
            link(V.tensor_tensor(wide, by_block(first_step, S), by_tile(iota_step[:], T), ALU.is_equal))
            begins = goes_on
            link(V.tensor_reduce(begins[:], wide, AX_X, ALU.add))
            link(V.tensor_copy(block_int[:], block_of[:]))
            loose(V.tensor_scalar(row_flag[:, 0:1], prow[:], float(R), None, ALU.is_equal))
            link(V.tensor_scalar(row_flag[:, 1:2], prow[:], float(R + 1), None, ALU.is_equal))
            link(V.tensor_tensor(row_flag[:, 2:3], row_flag[:, 0:1], row_flag[:, 1:2], ALU.add))
            link(V.tensor_scalar(row_flag[:, 3:4], row_flag[:, 1:2], float(T), float(N), ALU.mult, ALU.add))
            link(V.tensor_scalar(block_of[:], block_of[:], row_flag[:, 3:4], row_flag[:, 2:3], ALU.add, ALU.mult))
            dve.wait_ge(pick_done, 1)
            link(V.tensor_tensor(block_of[:], block_of[:], ps[:, 3, 0:S], ALU.add))
            loose(V.tensor_copy(slot_idx[:], block_of[:]))
            for h in range(2):
                loose(V.tensor_scalar(half_idx[:, h, :], block_of[:, 0:EARLY], 2.0, float(h), ALU.mult, ALU.add))
            loose(V.scalar_tensor_tensor(out=slot_gp[:], in0=begins[:], scalar=row_flag[:, 0:1], in1=ps[:, 3, S:2 * S],
                                         op0=ALU.mult, op1=ALU.add))
            link(V.scalar_tensor_tensor(out=slot_p[:], in0=begins[:], scalar=row_flag[:, 1:2],
                                        in1=ps[:, 3, 2 * S:3 * S], op0=ALU.mult, op1=ALU.add))
            V.tensor_scalar(goes_on[:], begins[:], -1.0, 1.0, ALU.mult, ALU.add).then_inc(slots_ok, 1)
            dve.wait_ge(slots_ok, 1)
            dve.wait_ge(table_loaded, 16)
            for c in range(C):
                V.tensor_tensor(diag[:, c * G:(c + 1) * G, :], ident[:].unsqueeze(1).broadcast_to((P, G, P)),
                                table[:, c * G:(c + 1) * G, COL_W:FX].broadcast_to((P, G, P)),
                                ALU.mult).then_inc(diag_ok, 1)
            dve.wait_ge(w_bc_ok, C)

            def den(s, k, first=False):
                if not first:
                    dve.wait_ge(num_done, (s - RING + 1) * C)
                J = block_reg(s)
                V.tensor_scalar(den_now[:, k, :], w_bc[:, bass.ds(J * P, P)], slot_gp[:, bass.ds(s, 1)],
                                slot_p[:, bass.ds(s, 1)], ALU.mult, ALU.max).then_inc(den_ok, 1)

            def block_reg(s):
                return V.value_load(block_int[0:1, bass.ds(s, 1)], min_val=0, max_val=T - 1)

            def add(s, c, J, n=1):
                dve.wait_ge(num_done, s * C + c + n)
                part = big[:, J, c * CH:(c + n) * CH]
                V.scalar_tensor_tensor(out=part, in0=part, scalar=goes_on[:, bass.ds(s, 1)],
                                       in1=ps[:, c:c + n, :].rearrange("p b n -> p (b n)"),
                                       op0=ALU.mult, op1=ALU.add).then_inc(num_added, n)

            def numer(J, h):
                V.tensor_scalar(att_num[:, h * H:(h + 1) * H], row_bc[:, h * H:(h + 1) * H],
                                table[:, J, COL_W:FX], 1.0,
                                ALU.mult, ALU.max).then_inc(numer_ok, 1)

            def att(J, h):
                dve.wait_ge(signed_ok, 2 * J + h + 1)
                dve.wait_ge(recip_ok, 2 * J + h + 1)
                half = big[:, J, h * H:(h + 1) * H]
                V.tensor_tensor(half, att_num[:, h * H:(h + 1) * H], square[:, h * H:(h + 1) * H],
                                ALU.mult).then_inc(att_ok, 1)

            def early_step(s, k):
                J = block_reg(s)
                for c in range(C):
                    add(s, c, J)
                den(s + RING, k)

            def late_step(s, k, first=False, last=False, fill=False):
                J = block_reg(s)
                if fill:
                    for c in range(C):
                        add(s, c, J)
                    den(s + RING, k)
                    for h in range(2):
                        if not first:
                            att(s - T - 1, h)
                            dve.wait_ge(att_ok, 2 * (s - T - 1) + h + 1)
                        numer(s - T, h)
                    return
                add(s, 0, J, 2)
                if not first:
                    att(s - T - 1, 0)
                add(s, 2, J, 2)
                if not first:
                    att(s - T - 1, 1)
                    dve.wait_ge(att_ok, 2 * (s - T - 1) + 1)
                numer(s - T, 0)
                if not first:
                    dve.wait_ge(att_ok, 2 * (s - T - 1) + 2)
                numer(s - T, 1)
                if not last:
                    den(s + RING, k)

            dve.wait_ge(w_bc_done, C + 1)
            for s in range(RING):
                den(s, s, True)
            for n in range(EARLY * C):
                h, s, c = early(n)
                dve.wait_ge(num_done, n + 1)
                if s:
                    dve.wait_ge(num_added, n - 1)
                J = block_reg(s)
                part = big[:, J, c * CH:(c + 1) * CH]
                V.scalar_tensor_tensor(out=part, in0=part, scalar=goes_on[:, bass.ds(s, 1)], in1=ps[:, n % C, :],
                                       op0=ALU.mult, op1=ALU.add).then_inc(num_added, 1)
            for s in range(EARLY):
                den(RING + s, s)
            for s in range(EARLY, RING):
                early_step(s, s)
            with dve.Fori(1, T // RING) as q:
                for k in range(RING):
                    early_step(q * RING + k, k)
            late_step(T, 0, first=True, fill=True)
            late_step(T + 1, 1, fill=True)
            late_step(T + 2, 2, fill=True)
            late_step(T + 3, 3)
            with dve.Fori(1, T // RING - 1) as q:
                for k in range(RING):
                    late_step(T + q * RING + k, k)
            for k in range(RING):
                late_step(S - RING + k, k, last=True)
            att(T - 1, 0)
            att(T - 1, 1)

            for c in range(C):
                dve.wait_ge(att_used, (T - 1) * C + c + 1)
                V.tensor_copy(sum_t[:, c * CH:(c + 1) * CH], ps[:, C + c, :]).then_inc(sum_t_sb, 1)
            for g in range(C):
                dve.wait_ge(sum_turned, g + 1)
                V.tensor_tensor(att_sum[:, g * G:(g + 1) * G, :], ps[:, g, :].rearrange("p (k f) -> p k f", k=G),
                                by_tile(p_nat[:, g * G:(g + 1) * G], P), ALU.mult).then_inc(sum_sb, 1)
            dve.wait_ge(x_loaded, 16)
            for c in range(C):
                dve.wait_ge(prod_turned, c + 1)
                if c >= 2:
                    dve.wait_ge(stored[c % 2], 16)
                V.tensor_tensor(result[:, c % 2], ps[:, c % 2, :].rearrange("p (k f) -> p k f", k=G),
                                x_again[:, c * G:(c + 1) * G, :], ALU.add).then_inc(res_ok, 1)


_INS = ["x", "adj", "L0_gnn_W", "L0_gnn_a"]


def kernel(**inputs):
    import numpy as _np
    import concourse.bacc as _bacc
    from concourse import mybir as _mybir
    from concourse.bass_utils import run_bass_kernel_spmd as _run

    nc = _bacc.Bacc("TRN2", target_bir_lowering=False, num_devices=1)
    arrays, args = {}, []
    for name in _INS:
        v = _np.ascontiguousarray(inputs[name])
        arrays[f"in_{name}"] = v
        args.append(nc.dram_tensor(f"in_{name}", v.shape, _mybir.dt.from_np(v.dtype), kind="ExternalInput").ap())
    out = nc.dram_tensor("out", inputs["x"].shape, _mybir.dt.float32, kind="ExternalOutput").ap()
    build_gnn(nc, *args, out)
    r = _run(nc, [arrays], core_ids=[0])
    return r.results[0]["out"]
```
